# Optimizing a Trainium2 kernel written in Bass

```python
import numpy as np
import jax
import jax.numpy as jnp

def _softmax(x, axis=-1):
    return jax.nn.softmax(x, axis=axis)

def _gelu(x):
    return jax.nn.gelu(x, approximate=True)

def _silu(x):
    return jax.nn.silu(x)

def _sigmoid(x):
    return jax.nn.sigmoid(x)

def _layernorm(x, axis=-1, eps=1e-05):
    m = jnp.mean(x, axis=axis, keepdims=True)
    v = jnp.var(x, axis=axis, keepdims=True)
    return (x - m) / jnp.sqrt(v + eps)

def _scatter_add(tgt, idx, src, axis=0):
    return tgt.at[idx].add(src)

def _segment_sum(src, seg, n):
    return jax.ops.segment_sum(src, seg, n)
kernel_name = 'mk_gnn_resnorm_d1_gnn_r64_a16d61'

def setup_inputs(seed: int=0):
    np.random.seed(seed)
    _w = jnp.asarray

    def _rec_inputs():
        import jax
        import jax.numpy as jnp
        _gk = jax.random.key(seed)
        x = -0.0003713 + 1 * jax.random.normal(jax.random.fold_in(_gk, 1), (50000, 256), jnp.float32)
        _s = jax.random.randint(jax.random.fold_in(_gk, 2), (12500,), 0, 50000, jnp.int32)
        _d = jax.random.randint(jax.random.fold_in(_gk, 3), (12500,), 0, 50000, jnp.int32)
        _loop = jnp.arange(50000, dtype=jnp.int32)
        src = jnp.concatenate([_s, _d, _loop])
        dst = jnp.concatenate([_d, _s, _loop])
        _o = jnp.argsort(dst, stable=True)
        src = src[_o]
        dst = dst[_o]
        return (x, src, dst)
    x, src, dst = _rec_inputs()

    def _L0_gnn_setup():
        import jax, jax.numpy as jnp
        import numpy as np
        N_NODES = 50000

        def _gcn_layer(h_in, W, b, src, dst, norm_edge, n_nodes):
            h = h_in @ W
            msg = h[src] * norm_edge[:, None]
            agg = jax.ops.segment_sum(msg, dst, num_segments=n_nodes)
            return agg + b
        key = jax.random.key(seed)
        ks = jax.random.split(key, 8)
        n, c_in, c_out = (N_NODES, 256, 256)
        hid = 2 * c_out
        E = 12500
        x = jax.random.normal(ks[0], (n, c_in), dtype=jnp.float32)
        edge_index = jax.random.randint(ks[1], (2, E), 0, n, dtype=jnp.int64)

        def glorot(k, fan_in, fan_out):
            s = jnp.sqrt(6.0 / (fan_in + fan_out)).astype(jnp.float32)
            return jax.random.uniform(k, (fan_in, fan_out), jnp.float32, -s, s)
        return {'x': x, 'edge_index': edge_index, 'W1': glorot(ks[2], c_in, hid), 'b1': jnp.zeros((hid,), jnp.float32), 'W2': glorot(ks[3], hid, hid), 'b2': jnp.zeros((hid,), jnp.float32), 'W3': glorot(ks[4], hid, c_out), 'b3': jnp.zeros((c_out,), jnp.float32)}
    _L0_gnn_all = _L0_gnn_setup()
    _L0_gnn_in = {k: v for k, v in _L0_gnn_all.items() if k in ('W1', 'b1', 'W2', 'b2', 'W3', 'b3')}
    del _L0_gnn_all
    return {'x': x, 'src': src, 'dst': dst, 'L0_gnn_W1': _L0_gnn_in['W1'], 'L0_gnn_b1': _L0_gnn_in['b1'], 'L0_gnn_W2': _L0_gnn_in['W2'], 'L0_gnn_b2': _L0_gnn_in['b2'], 'L0_gnn_W3': _L0_gnn_in['W3'], 'L0_gnn_b3': _L0_gnn_in['b3']}

def reference(x, src, dst, L0_gnn_W1, L0_gnn_b1, L0_gnn_W2, L0_gnn_b2, L0_gnn_W3, L0_gnn_b3):
    import jax
    import jax.numpy as jnp

    def _L0_gnn_ref(x, edge_index, W1, b1, W2, b2, W3, b3):
        import jax, jax.numpy as jnp
        import numpy as np
        N_NODES = 50000

        def _gcn_layer(h_in, W, b, src, dst, norm_edge, n_nodes):
            h = h_in @ W
            msg = h[src] * norm_edge[:, None]
            agg = jax.ops.segment_sum(msg, dst, num_segments=n_nodes)
            return agg + b
        n = x.shape[0]
        loops = jnp.arange(n, dtype=edge_index.dtype)
        src = jnp.concatenate([edge_index[0], loops])
        dst = jnp.concatenate([edge_index[1], loops])
        deg = jax.ops.segment_sum(jnp.ones_like(dst, dtype=x.dtype), dst, num_segments=n)
        dinv = jnp.where(deg > 0, jax.lax.rsqrt(deg), 0.0)
        norm_edge = dinv[src] * dinv[dst]
        h = x
        for W, b in ((W1, b1), (W2, b2), (W3, b3)):
            h = jax.nn.relu(_gcn_layer(h, W, b, src, dst, norm_edge, n))
        return h
    edge_index = jnp.stack([src, dst])
    x = _layernorm(x + _L0_gnn_ref(x, edge_index, L0_gnn_W1, L0_gnn_b1, L0_gnn_W2, L0_gnn_b2, L0_gnn_W3, L0_gnn_b3), axis=-1)
    return x

_drawn_inputs = setup_inputs


def setup_inputs(seed=0):
    import zlib

    import numpy as np

    out = dict(_drawn_inputs(seed))
    spreads = {'L0_gnn_b1': (0.0, 0.1), 'L0_gnn_b2': (0.0, 0.1), 'L0_gnn_b3': (0.0, 0.1)}
    factors = {}
    for name, (base, spread) in spreads.items():
        noise = np.random.default_rng([zlib.crc32(name.encode()), seed]).standard_normal(out[name].shape)
        drawn = base * np.exp(spread * noise) if base else spread * noise
        out[name] = jnp.asarray(drawn.astype(out[name].dtype))
    for name, factor in factors.items():
        out[name] = (out[name] * factor).astype(out[name].dtype)
    return out
```

```python
from contextlib import ExitStack

import concourse.bass as bass
from concourse import mybir

ALU = mybir.AluOpType
ACT = mybir.ActivationFunctionType
AX = mybir.AxisListType
F32 = mybir.dt.float32
F32R = mybir.dt.float32r
BF16 = mybir.dt.bfloat16
I32 = mybir.dt.int32

P = 128
TS = 4
BLK = 125
WBLK = 3
WIN = WBLK * BLK
SLOTS = 128
ROUNDS = 14
RELBIT = 16
CHUNK = 125
EPS = 1e-5
FAR = 1000000.0


def gnn_kernel(nc, x, src, dst, W1, b1, W2, b2, W3, b3, out):
    N, C = x.shape
    E = src.shape[0]
    H = W1.shape[1]
    NS = -(-N // (TS * P))
    NT = NS * TS
    NP = NT * P
    NB = E // BLK
    NCH = E // CHUNK
    KC, KH = C // P, H // P
    TAIL = N - (NS - 1) * TS * P
    TF, TR = TAIL // P, TAIL % P
    assert E % BLK == 0 and E % (2 * CHUNK) == 0 and NB % 2 == 0 and NB <= 1024 and N < 1 << RELBIT and NS <= P
    assert TR % 16 == 0 and TR and H == 512 and C == 256

    def dram(name, shape, dt=F32):
        return nc.dram_tensor(name, shape, dt, kind="Internal").ap()

    h1_table = dram("h1_table", (NP, H))
    z_table = dram("z_table", (NP, C))
    dinv_table = dram("dinv_table", (NP, 1))
    weight_table = dram("weight_table", (NP, 1))
    count_table = dram("count_table", (NP, 1))
    sum_table = dram("sum_table", (NP, H))
    sum_half = sum_table.rearrange("n (a c) -> (n a) c", a=H // C)[0:NP, :]

    top = ExitStack()

    def sb(ctx, name, shape, dt=F32):
        return ctx.enter_context(nc.sbuf_tensor(name, shape, dt))

    def ps(ctx, name, shape, dt=F32):
        return ctx.enter_context(nc.psum_tensor(name, shape, dt))

    def sem(name):
        return top.enter_context(nc.semaphore(name))

    with top:
        w1 = [sb(top, f"w1_{h}", [P, KC, H], F32R) for h in ("hi", "lo")]
        w2 = [sb(top, f"w2_{h}", [P, KH, H], F32R) for h in ("hi", "lo")]
        w3 = [sb(top, f"w3_{h}", [P, KH, C], F32R) for h in ("hi", "lo")]
        b1_rows = sb(top, "b1_rows", [P, H], F32R)
        ones_rows = sb(top, "ones_rows", [P, P], F32R)
        b2_cols = sb(top, "b2_cols", [P, KH])
        b3_all = sb(top, "b3_all", [P, C])
        ident = sb(top, "ident", [P, P])
        iota_free = sb(top, "iota_free", [P, P])
        iota_part = sb(top, "iota_part", [P, 1])
        slot_src = sb(top, "slot_src", [P, NT], I32)
        slot_rel = sb(top, "slot_rel", [P, NT])
        dinv = sb(top, "dinv", [P, NT])
        self1 = sb(top, "self1", [P, NT])
        self23 = sb(top, "self23", [P, NT])
        fast = sb(top, "fast", [P, 2])
        general_flag = sb(top, "general_flag", [P, 1], I32)
        own_factor = sb(top, "own_factor", [P, 1])


        def make_slots():
            with ExitStack() as ctx:
                first_i = sb(ctx, "first_i", [1, NB], I32)
                first_f = sb(ctx, "first_f", [1, NB])
                ones_f = sb(ctx, "ones_f", [P, P])
                stage = sb(ctx, "stage", [P, KH, H])
                stage3 = sb(ctx, "stage3", [P, KH, C])
                stage1 = sb(ctx, "stage1", [P, KC, H])
                bias_f = sb(ctx, "bias_f", [P, H])
                rows_f = sb(ctx, "rows_f", [P, P])
                node0 = sb(ctx, "node0", [P, TS])
                below = sb(ctx, "below", [P, NB])
                nbelow = sb(ctx, "nbelow", [P, TS])
                block_f = sb(ctx, "block_f", [P, TS])
                block_i = sb(ctx, "block_i", [P, WBLK, TS], I32)
                win_dst_i = sb(ctx, "win_dst_i", [P, TS, WIN], I32)
                win_src_i = sb(ctx, "win_src_i", [P, TS, WIN], I32)
                win_dst = sb(ctx, "win_dst", [P, TS, WIN])
                win_src = sb(ctx, "win_src", [P, TS, WIN])
                rel = sb(ctx, "rel", [P, TS, WIN])
                inside = sb(ctx, "inside", [P, TS, WIN])
                tmp = sb(ctx, "tmp", [P, TS, WIN])
                same = sb(ctx, "same", [P, TS, WIN])
                selfs = sb(ctx, "selfs", [P, TS, WIN])
                key = sb(ctx, "key", [P, TS, WIN])
                slot_key = sb(ctx, "slot_key", [P, TS, SLOTS])
                kept = sb(ctx, "kept", [P, TS])
                stats = sb(ctx, "stats", [P, 4])
                verdict = sb(ctx, "verdict", [P, 4])
                node_id = sb(ctx, "node_id", [P, NT])
                node_mix = sb(ctx, "node_mix", [P, NT])
                part_mix = sb(ctx, "part_mix", [P, 1])
                key_i = sb(ctx, "key_i", [P, NT], I32)
                low_i = sb(ctx, "low_i", [P, NT], I32)
                high_i = sb(ctx, "high_i", [P, NT], I32)
                src_f = sb(ctx, "src_f", [P, NT])
                rel_f = sb(ctx, "rel_f", [P, NT])
                ps_first = ps(ctx, "ps_first", [P, 2, 512])
                ps_stats = ps(ctx, "ps_stats", [P, 4])
                ps_keys = ps(ctx, "ps_keys", [P, TS, NS])
                first_loaded, weights_loaded, bias_loaded = sem("first_loaded"), sem("weights_loaded"), sem("bias_loaded")
                iotas_ready, zeros_ready, first_ready = sem("iotas_ready"), sem("zeros_ready"), sem("first_ready")
                first_spread, blocks_ready = sem("first_spread"), sem("blocks_ready")
                dst_windows, src_windows = sem("dst_windows"), sem("src_windows")
                halves_ready, stats_ready, stats_summed = sem("halves_ready"), sem("stats_ready"), sem("stats_summed")
                keys_ready, keys_turned, prep_chain = sem("keys_ready"), sem("keys_turned"), sem("prep_chain")
                block = ctx.enter_context(nc.Block())

                @block.sync
                def _(sp):
                    with nc.allow_non_contiguous_dma(reason="the first edge of each block"):
                        sp.dma_start(first_i[:], dst.rearrange("(o b k) -> o b k", o=1, k=BLK)[:, :, 0]).then_inc(first_loaded, 16)
                    sp.dma_start(stage1[:], W1.rearrange("(k p) n -> p k n", p=P)).then_inc(weights_loaded, 16)
                    sp.dma_start(stage[:], W2.rearrange("(k p) n -> p k n", p=P)).then_inc(weights_loaded, 16)
                    sp.dma_start(stage3[:], W3.rearrange("(k p) n -> p k n", p=P)).then_inc(weights_loaded, 16)
                    sp.dma_start(b3_all[:], b3.rearrange("(o n) -> o n", o=1).to_broadcast([P, C])).then_inc(weights_loaded, 16)
                    with nc.allow_non_contiguous_dma(reason="512 biases, features on partitions"):
                        sp.dma_start(b2_cols[:], b2.rearrange("(f p) -> p f", p=P)).then_inc(weights_loaded, 16)
                    sp.wait_ge(zeros_ready, 1)
                    for row in (0, 32):
                        sp.dma_start(bias_f[row:row + 1, :], b1.rearrange("(o n) -> o n", o=1)).then_inc(bias_loaded, 16)

                @block.gpsimd
                def _(pool):
                    pool.iota(node0[:], [[P, TS]], base=0, channel_multiplier=TS * P, allow_small_or_imprecise_dtypes=True)
                    pool.iota(iota_free[:], [[1, P]], base=0, channel_multiplier=0, allow_small_or_imprecise_dtypes=True)
                    pool.iota(iota_part[:], [[0, 1]], base=0, channel_multiplier=1, allow_small_or_imprecise_dtypes=True)
                    pool.iota(node_id[:], [[P, NT]], base=0, channel_multiplier=1,
                              allow_small_or_imprecise_dtypes=True).then_inc(iotas_ready, 1)
                    pool.memset(win_dst_i[:], 0)
                    pool.memset(win_src_i[:], 0).then_inc(iotas_ready, 1)
                    pool.wait_ge(iotas_ready, 2)
                    pool.wait_ge(blocks_ready, 1)
                    for edges, window, done in ((dst, win_dst_i, dst_windows), (src, win_src_i, src_windows)):
                        blocks = edges.rearrange("(b k) -> b k", k=BLK)
                        for g in range(TS):
                            for h in range(WBLK):
                                pool.indirect_dma_start(
                                    window[0:NS, g, h * BLK:(h + 1) * BLK], None, blocks,
                                    bass.IndirectOffsetOnAxis(ap=block_i[0:NS, h, g:g + 1], axis=0),
                                    bounds_check=NB - 1, oob_is_err=False).then_inc(done, 16)

                @block.scalar
                def _(act):
                    act.wait_ge(weights_loaded, 80)
                    act.activation(w1[0][:], stage1[:], ACT.Copy)
                    act.activation(w2[0][:], stage[:], ACT.Copy)
                    act.activation(w3[0][:], stage3[:], ACT.Copy).then_inc(halves_ready, 1)
                    act.wait_ge(bias_loaded, 32)
                    act.activation(b1_rows[:], bias_f[:], ACT.Copy).then_inc(halves_ready, 1)
                    act.wait_ge(zeros_ready, 3)
                    act.activation(ones_rows[:], rows_f[:], ACT.Copy)

                @block.tensor
                def _(pe):
                    pe.wait_ge(first_ready, 1)
                    for h in range(2):
                        last = pe.matmul(ps_first[:, h, 0:NB // 2], ones_f[0:1, :], first_f[:, h * NB // 2:(h + 1) * NB // 2], start=True, stop=True)
                    last.then_inc(first_spread, 1)
                    pe.wait_ge(stats_ready, 1)
                    pe.matmul(ps_stats[:], ones_f[:], stats[:], start=True, stop=True).then_inc(stats_summed, 1)
                    pe.wait_ge(keys_ready, 1)
                    for g in range(TS):
                        last = pe.transpose(ps_keys[:, g, :], slot_key[0:NS, g, :], ident[0:NS, 0:NS])
                    last.then_inc(keys_turned, 1)

                @block.vector
                def _(dve):
                    count = [0]

                    def link(ins):
                        count[0] += 1
                        ins.then_inc(prep_chain, 1)
                        dve.wait_ge(prep_chain, count[0])

                    dve.memset(bias_f[:], 0.0).then_inc(zeros_ready, 1)
                    dve.memset(stats[:], 0.0)
                    dve.memset(slot_key[:], 0.0)
                    dve.memset(ones_f[:], 1.0)
                    dve.memset(rows_f[:], 0.0).then_inc(zeros_ready, 1)
                    dve.wait_ge(zeros_ready, 2)
                    dve.memset(rows_f[0:1, :], 1.0)
                    dve.memset(rows_f[32:33, :], 1.0).then_inc(zeros_ready, 1)
                    dve.wait_ge(first_loaded, 16)
                    dve.tensor_copy(first_f[:], first_i[:]).then_inc(first_ready, 1)
                    dve.wait_ge(iotas_ready, 1)
                    link(dve.tensor_scalar(ident[:], iota_free[:], iota_part[:], None, ALU.is_equal))
                    dve.wait_ge(first_spread, 1)
                    for g in range(TS):
                        link(dve.tensor_scalar(below[:].rearrange("p (h b) -> p h b", h=2), ps_first[:, :, 0:NB // 2], node0[:, g:g + 1], None, ALU.is_lt))
                        link(dve.tensor_reduce(nbelow[:, g:g + 1], below[:], AX.X, ALU.add))
                    link(dve.tensor_scalar(block_f[:], nbelow[:], -1.0, 0.0, ALU.add, ALU.max))
                    link(dve.tensor_scalar(block_f[:], block_f[:], float(NB - WBLK), None, ALU.min))
                    for h in range(WBLK):
                        link(dve.tensor_scalar(block_i[:, h, :], block_f[:], float(h), None, ALU.add))
                    dve.sem_inc(blocks_ready, 1)
                    dve.wait_ge(halves_ready, 2)
                    dve.tensor_tensor(w1[1][:], stage1[:], w1[0][:].bitcast(F32), ALU.subtract)
                    dve.tensor_tensor(w2[1][:], stage[:], w2[0][:].bitcast(F32), ALU.subtract)
                    dve.tensor_tensor(w3[1][:], stage3[:], w3[0][:].bitcast(F32), ALU.subtract)
                    dve.tensor_tensor(b1_rows[32:33, :], bias_f[32:33, :], b1_rows[32:33, :].bitcast(F32), ALU.subtract)
                    dve.wait_ge(dst_windows, 16 * WBLK * TS)
                    link(dve.tensor_copy(win_dst[:], win_dst_i[:]))
                    for g in range(TS):
                        link(dve.tensor_scalar(rel[:, g, :], win_dst[:, g, :], node0[:, g:g + 1], None, ALU.subtract))
                    link(dve.tensor_scalar(inside[:], rel[:], 0.0, None, ALU.is_ge))
                    link(dve.scalar_tensor_tensor(inside[:], rel[:], float(P), inside[:], ALU.is_lt, ALU.mult))
                    link(dve.memset(same[:], 0.0))
                    link(dve.tensor_tensor(same[:, :, 1:WIN], win_dst[:, :, 1:WIN], win_dst[:, :, 0:WIN - 1], ALU.is_equal))
                    link(dve.memset(tmp[:], 0.0))
                    link(dve.tensor_tensor(tmp[:, :, 1:WIN], win_dst[:, :, 1:WIN], win_dst[:, :, 0:WIN - 1], ALU.is_lt))
                    link(dve.tensor_reduce(stats[0:NS, 2:3], tmp[0:NS].rearrange("p g w -> p (g w)"), AX.X, ALU.add))
                    dve.wait_ge(src_windows, 16 * WBLK * TS)
                    link(dve.tensor_copy(win_src[:], win_src_i[:]))
                    link(dve.tensor_tensor(selfs[:], win_dst[:], win_src[:], ALU.is_equal))
                    link(dve.tensor_tensor(selfs[:], selfs[:], inside[:], ALU.mult))
                    link(dve.tensor_tensor_scan(tmp[:].rearrange("p g w -> p (g w)"), same[:].rearrange("p g w -> p (g w)"),
                                                selfs[:].rearrange("p g w -> p (g w)"), 0.0, ALU.mult, ALU.add))
                    link(dve.scalar_tensor_tensor(selfs[:], tmp[:], 1.0, selfs[:], ALU.is_equal, ALU.mult))
                    link(dve.tensor_reduce(stats[0:NS, 1:2], selfs[0:NS].rearrange("p g w -> p (g w)"), AX.X, ALU.add))
                    link(dve.tensor_reduce(stats[0:NS, 0:1], inside[0:NS].rearrange("p g w -> p (g w)"), AX.X, ALU.add))
                    link(dve.tensor_tensor(inside[:], inside[:], selfs[:], ALU.subtract))
                    link(dve.tensor_reduce(kept[:], inside[:], AX.X, ALU.add))
                    link(dve.tensor_scalar(kept[:], kept[:], float(8 * ROUNDS), None, ALU.is_gt))
                    link(dve.tensor_reduce(stats[0:NS, 3:4], kept[0:NS, :], AX.X, ALU.add))
                    dve.sem_inc(stats_ready, 1)
                    link(dve.scalar_tensor_tensor(key[:], rel[:], float(1 << RELBIT), win_src[:], ALU.mult, ALU.add))
                    link(dve.scalar_tensor_tensor(key[:], key[:], 1.0, inside[:], ALU.add, ALU.mult))
                    for r in range(ROUNDS):
                        for g in range(TS):
                            top8 = slot_key[0:NS, g, 8 * r:8 * r + 8]
                            link(dve.max(top8, key[0:NS, g, :]))
                            if r < ROUNDS - 1:
                                link(dve.match_replace(key[0:NS, g, :], top8, key[0:NS, g, :], 0.0))
                    dve.sem_inc(keys_ready, 1)
                    dve.wait_ge(stats_summed, 1)
                    link(dve.tensor_scalar(verdict[:, 0:1], ps_stats[:, 0:1], float(E), None, ALU.is_equal))
                    link(dve.tensor_scalar(verdict[:, 1:2], ps_stats[:, 1:2], float(N), None, ALU.is_equal))
                    link(dve.tensor_scalar(verdict[:, 2:4], ps_stats[:, 2:4], 0.0, None, ALU.is_equal))
                    link(dve.tensor_reduce(fast[:, 0:1], verdict[:], AX.X, ALU.min))
                    link(dve.tensor_scalar(fast[:, 1:2], fast[:, 0:1], -1.0, 1.0, ALU.mult, ALU.add))
                    link(dve.tensor_copy(general_flag[:], fast[:, 1:2]))
                    dve.wait_ge(keys_turned, 1)
                    link(dve.tensor_scalar(key_i[:].rearrange("p (s g) -> p g s", g=TS), ps_keys[:], -1.0, None, ALU.add))
                    link(dve.tensor_scalar(low_i[:], key_i[:], (1 << RELBIT) - 1, None, ALU.bitwise_and))
                    link(dve.tensor_scalar(high_i[:], key_i[:], RELBIT, None, ALU.logical_shift_right))
                    link(dve.tensor_copy(src_f[:], low_i[:]))
                    link(dve.tensor_copy(rel_f[:], high_i[:]))
                    link(dve.tensor_scalar(node_mix[:], node_id[:], fast[:, 1:2], None, ALU.mult))
                    link(dve.tensor_scalar(part_mix[:], iota_part[:], fast[:, 1:2], None, ALU.mult))
                    link(dve.scalar_tensor_tensor(slot_src[:], src_f[:], fast[:, 0:1], node_mix[:], ALU.mult, ALU.add))
                    link(dve.tensor_scalar(slot_rel[:], rel_f[:], fast[:, 0:1], part_mix[:], ALU.mult, ALU.add))

        def make_degrees():
            with ExitStack() as ctx:
                one_hot = sb(ctx, "one_hot", [P, 2, TS, P], BF16)
                ones_b = sb(ctx, "ones_b", [P, 1], BF16)
                iota_b = sb(ctx, "iota_b", [P, P], BF16)
                slot_rel_b = sb(ctx, "slot_rel_b", [P, NT], BF16)
                degree = sb(ctx, "degree", [P, NT])
                root = sb(ctx, "root", [P, NT])
                counted = sb(ctx, "counted", [P, TS, P])
                weight = sb(ctx, "weight", [P, NT])
                turned = sb(ctx, "turned", [P, 2, TS, P])
                ps_count = ps(ctx, "ps_count", [P, NT])
                ps_general = ps(ctx, "ps_general", [P, TS, P])
                ps_dinv = ps(ctx, "ps_dinv", [P, TS, P])
                ps_weight = ps(ctx, "ps_weight", [P, TS, P])
                hot_ready, tiles_counted = sem("hot_ready"), sem("tiles_counted")
                general_loaded, general_turned, counts_present = sem("general_loaded"), sem("general_turned"), sem("counts_present")
                counted_zeroed, degree_ready, root_ready = sem("counted_zeroed"), sem("degree_ready"), sem("root_ready")
                dinv_ready, dinv_turned, dinv_copied = sem("dinv_ready"), sem("dinv_turned"), sem("dinv_copied")
                tables_stored, degree_chain, ones_b_ready = sem("tables_stored"), sem("degree_chain"), sem("ones_b_ready")
                block = ctx.enter_context(nc.Block())

                @block.sync
                def _(sp):
                    sp.wait_ge(counted_zeroed, 1)
                    general = sp.value_load(general_flag[0:1, 0:1], min_val=0, max_val=1)
                    with sp.If(general == 1):
                        sp.dma_start(counted[0:NS], count_table.rearrange("(s g p) o -> s g (p o)", g=TS, p=P)).then_inc(general_loaded, 16)
                        sp.wait_ge(general_loaded, 16)
                    sp.sem_inc(counts_present, 1)
                    sp.wait_ge(dinv_copied, 2)
                    for k, table in enumerate((dinv_table, weight_table)):
                        sp.dma_start(table.rearrange("(s g p) o -> s g (p o)", g=TS, p=P), turned[0:NS, k]).then_inc(tables_stored, 16)
                    sp.wait_ge(tables_stored, 32)

                @block.vector
                def _(dve):
                    count = [0]

                    def link(ins):
                        count[0] += 1
                        ins.then_inc(degree_chain, 1)
                        dve.wait_ge(degree_chain, count[0])

                    dve.memset(counted[:], 0.0).then_inc(counted_zeroed, 1)
                    dve.memset(ones_b[:], 1.0).then_inc(ones_b_ready, 1)
                    link(dve.tensor_copy(iota_b[:], iota_free[:]))
                    link(dve.tensor_copy(slot_rel_b[:], slot_rel[:]))
                    link(dve.tensor_scalar(own_factor[:], fast[:, 0:1], 1.0, None, ALU.add))

                    def hot(sup, q):
                        dve.tensor_tensor(
                            one_hot[:, q], iota_b[:].rearrange("p (o n) -> p o n", o=1).to_broadcast([P, TS, P]),
                            slot_rel_b[:, bass.ts(sup, TS)].rearrange("p (g o) -> p g o", o=1).to_broadcast([P, TS, P]),
                            ALU.is_equal).then_inc(hot_ready, 1)

                    hot(0, 0)
                    hot(1, 1)
                    with dve.Fori(1, NS // 2) as i:
                        for q in range(2):
                            dve.wait_ge(tiles_counted, 2 * i + q - 1)
                            hot(2 * i + q, q)
                    dve.wait_ge(tiles_counted, NS)
                    link(dve.tensor_scalar(degree[:], ps_count[:], fast[:, 0:1], own_factor[:], ALU.mult, ALU.add))
                    dve.wait_ge(general_turned, 1)
                    link(dve.scalar_tensor_tensor(degree[:].rearrange("p (s g) -> p g s", g=TS), ps_general[:, :, 0:NS], fast[:, 1:2],
                                                  degree[:].rearrange("p (s g) -> p g s", g=TS), ALU.mult, ALU.add))
                    dve.sem_inc(degree_ready, 1)
                    dve.wait_ge(root_ready, 1)
                    link(dve.reciprocal(dinv[:], root[:]))
                    link(dve.tensor_tensor(dinv[:], degree[:], dinv[:], ALU.mult))
                    link(dve.tensor_tensor(root[:], root[:], dinv[:], ALU.add))
                    link(dve.reciprocal(dinv[:], root[:]))
                    link(dve.tensor_scalar(dinv[:], dinv[:], 2.0, None, ALU.mult))
                    link(dve.tensor_scalar(self23[:], dinv[:], own_factor[:], None, ALU.mult))
                    link(dve.tensor_tensor(self1[:], self23[:], dinv[:], ALU.mult))
                    link(dve.tensor_scalar(weight[:], dinv[:], fast[:, 0:1], fast[:, 1:2], ALU.mult, ALU.add))
                    dve.sem_inc(dinv_ready, 1)
                    dve.wait_ge(dinv_turned, 1)
                    dve.tensor_copy(turned[0:NS, 0], ps_dinv[0:NS]).then_inc(dinv_copied, 1)
                    dve.tensor_copy(turned[0:NS, 1], ps_weight[0:NS]).then_inc(dinv_copied, 1)

                @block.scalar
                def _(act):
                    act.wait_ge(degree_ready, 1)
                    act.activation(root[:], degree[:], ACT.Sqrt).then_inc(root_ready, 1)

                @block.tensor
                def _(pe):
                    pe.wait_ge(ones_b_ready, 1)
                    with pe.Fori(0, NS // 2) as i:
                        for q in range(2):
                            pe.wait_ge(hot_ready, 2 * i + q + 1)
                            for g in range(TS):
                                last = pe.matmul(ps_count[:, bass.ds(2 * TS * i + TS * q + g, 1)], one_hot[:, q, g, :], ones_b[:],
                                                 start=True, stop=True)
                            last.then_inc(tiles_counted, 1)
                    pe.wait_ge(counts_present, 1)
                    for g in range(TS):
                        last = pe.transpose(ps_general[:, g, 0:NS], counted[0:NS, g, :], ident[0:NS, 0:NS])
                    last.then_inc(general_turned, 1)
                    pe.wait_ge(dinv_ready, 1)
                    for g in range(TS):
                        pe.transpose(ps_dinv[0:NS, g, :], dinv[:].rearrange("p (s g) -> p g s", g=TS)[:, g, :], ident[:])
                        last = pe.transpose(ps_weight[0:NS, g, :], weight[:].rearrange("p (s g) -> p g s", g=TS)[:, g, :], ident[:])
                    last.then_inc(dinv_turned, 1)

        def loops(body):
            supers = body // TS

            def exists(i, k):
                return not isinstance(i, int) or 0 <= body * i + k < NT

            def follows(i, k, n):
                return not isinstance(i, int) or body * i + k >= n

            def tile_loop(engine, step, ahead=0, behind=0):
                plain, end = 2 if behind else 1, (NT - ahead) // body
                for k in range(-ahead, 0):
                    step(0, k)
                for m in range(plain * body):
                    step(m // body, m % body)
                with engine.Fori(plain, end) as i:
                    for k in range(body):
                        step(i, k)
                for m in range(end * body, NT + behind):
                    step(end, m - end * body)

            def super_loop(engine, step, plain=1):
                end = (NS - 1) // supers
                for n in range(plain * supers):
                    step(n // supers, n % supers)
                with engine.Fori(plain, end) as i:
                    for j in range(supers):
                        step(i, j)
                for n in range(end * supers, NS):
                    step(end, n - end * supers)

            return exists, follows, tile_loop, super_loop

        def super_rows(table, s):
            return table[bass.ds(s * TS * P, TS * P), :].rearrange("(j p) c -> p j c", p=P)

        LAST = (NS - 1) * TS * P

        def load_tail(sp, buffer, table, loaded, tail_loaded):
            sp.dma_start(buffer[0:TR, TF, :], table[LAST + TF * P:N, :]).then_inc(tail_loaded, 16)
            sp.wait_ge(tail_loaded, 16)
            sp.dma_start(buffer[:, 0:TF, :], table[LAST:LAST + TF * P, :].rearrange("(j p) c -> p j c", p=P)).then_inc(loaded, 16)

        edges_loaded, sums_cleared, constants_ready = sem("edges_loaded"), sem("sums_cleared"), sem("constants_ready")
        wide_ready, wide_turned, equal_ready = sem("wide_ready"), sem("wide_turned"), sem("equal_ready")
        repeats_ready, count_ready, write_ready = sem("repeats_ready"), sem("count_ready"), sem("write_ready")
        chunk_rows_gathered, chunk_weights_gathered, old_gathered = sem("chunk_rows_gathered"), sem("chunk_weights_gathered"), sem("old_gathered")
        rows_scaled, new_ready = sem("rows_scaled"), sem("new_ready")
        total_ready, chunk_scattered, pool_step = sem("total_ready"), sem("chunk_scattered"), sem("pool_step")

        def general_sums(tag, turn, width, table, weighted, sums, rows_before=0):
            with ExitStack() as ctx:
                src_all = sb(ctx, f"src_all_{tag}", [CHUNK, NCH], I32)
                dst_all = sb(ctx, f"dst_all_{tag}", [CHUNK, NCH], I32)
                dst_f = sb(ctx, f"dst_f_{tag}", [CHUNK, NCH])
                zeros = sb(ctx, f"zeros_{tag}", [P, TS, width])
                before = sb(ctx, f"before_{tag}", [CHUNK, CHUNK])
                dst_wide = sb(ctx, f"dst_wide_{tag}", [CHUNK, CHUNK])
                equal = sb(ctx, f"equal_{tag}", [CHUNK, CHUNK])
                repeats = sb(ctx, f"repeats_{tag}", [CHUNK, CHUNK])
                n_before = sb(ctx, f"n_before_{tag}", [CHUNK, 1])
                src_col = sb(ctx, f"src_col_{tag}", [CHUNK, 1], I32)
                dst_col = sb(ctx, f"dst_col_{tag}", [CHUNK, 1], I32)
                write_col = sb(ctx, f"write_col_{tag}", [CHUNK, 2], I32)
                rows = sb(ctx, f"rows_{tag}", [CHUNK, width])
                row_weight = sb(ctx, f"row_weight_{tag}", [CHUNK, 1])
                old = sb(ctx, f"old_{tag}", [CHUNK, width])
                total = sb(ctx, f"total_{tag}", [CHUNK, width])
                ps_dst = ps(ctx, f"ps_dst_{tag}", [CHUNK, CHUNK])
                ps_new = ps(ctx, f"ps_new_{tag}", [CHUNK, width])
                chunk0 = turn * NCH
                block = ctx.enter_context(nc.Block())

                @block.sync
                def _(sp):
                    general = sp.value_load(general_flag[0:1, 0:1], min_val=0, max_val=1)
                    with sp.If(general == 1):
                        sp.dma_start(src_all[:], src.rearrange("(p c) -> p c", p=CHUNK)).then_inc(edges_loaded, 16)
                        sp.dma_start(dst_all[:], dst.rearrange("(p c) -> p c", p=CHUNK)).then_inc(edges_loaded, 16)
                        sp.wait_ge(constants_ready, 2 * turn + 1)
                        with sp.Fori(0, NS) as s:
                            sp.dma_start(sums[bass.ds(s * TS * P, TS * P), :].rearrange("(p j) c -> p j c", p=P), zeros[:]).then_inc(sums_cleared, 16)
                        sp.wait_ge(sums_cleared, 16 * NS * (turn + 1))

                @block.gpsimd
                def _(pool):
                    general = pool.value_load(general_flag[0:1, 0:1], min_val=0, max_val=1)
                    bounds = {n: pool.to_reg(n - 1) for n in (N, NP)}

                    def gather(buffer, source, n, index, done):
                        pool.indirect_dma_start(buffer, None, source, bass.IndirectOffsetOnAxis(ap=index, axis=0),
                                                bounds_check=bounds[n], oob_is_err=False).then_inc(done, 16)

                    with pool.If(general == 1):
                        pool.wait_ge(sums_cleared, 16 * NS * (turn + 1))
                        with pool.Fori(0, NCH // 2) as i:
                            for k in range(2):
                                pool.wait_ge(write_ready, chunk0 + 2 * i + k + 1)
                                pool.sem_inc(pool_step, 1)
                                if table is not None:
                                    gather(rows[:], table, N, src_col[:], chunk_rows_gathered)
                                if weighted:
                                    gather(row_weight[:], dinv_table, NP, src_col[:], chunk_weights_gathered)
                                gather(old[:], sums, NP, dst_col[:], old_gathered)
                                pool.wait_ge(total_ready, chunk0 + 2 * i + k + 1)
                                pool.sem_inc(pool_step, 1)
                                pool.indirect_dma_start(sums, bass.IndirectOffsetOnAxis(ap=write_col[:, k:k + 1], axis=0), total[:], None,
                                                        bounds_check=bounds[NP], oob_is_err=False).then_inc(chunk_scattered, 16)
                                pool.wait_ge(chunk_scattered, 16 * (chunk0 + 2 * i + k + 1))
                                pool.sem_inc(pool_step, 1)

                @block.vector
                def _(dve):
                    general = dve.value_load(general_flag[0:1, 0:1], min_val=0, max_val=1)
                    with dve.If(general == 1):
                        dve.memset(rows[:], 1.0)
                        dve.tensor_scalar(before[:], iota_free[0:CHUNK, 0:CHUNK], iota_part[0:CHUNK, :], None, ALU.is_lt)
                        dve.memset(zeros[:], 0.0).then_inc(constants_ready, 1)
                        dve.wait_ge(edges_loaded, 32 * (turn + 1))
                        dve.tensor_copy(dst_f[:], dst_all[:]).then_inc(constants_ready, 1)
                        dve.wait_ge(constants_ready, 2 * turn + 2)
                        with dve.Fori(0, NCH // 2) as i:
                            for k in range(2):
                                c = 2 * i + k
                                this_dst = dst_f[:, bass.ds(c, 1)]
                                dve.tensor_copy(dst_wide[:], this_dst.to_broadcast([CHUNK, CHUNK])).then_inc(wide_ready, 1)
                                dve.tensor_copy(src_col[:], src_all[:, bass.ds(c, 1)])
                                dve.tensor_copy(dst_col[:], dst_all[:, bass.ds(c, 1)])
                                dve.wait_ge(wide_turned, chunk0 + c + 1)
                                dve.tensor_scalar(equal[:], ps_dst[:], this_dst, None, ALU.is_equal).then_inc(equal_ready, 1)
                                dve.wait_ge(equal_ready, chunk0 + c + 1)
                                dve.tensor_tensor(repeats[:], equal[:], before[:], ALU.mult).then_inc(repeats_ready, 1)
                                dve.wait_ge(repeats_ready, chunk0 + c + 1)
                                dve.tensor_reduce(n_before[:], repeats[:], AX.X, ALU.add).then_inc(count_ready, 1)
                                dve.wait_ge(count_ready, chunk0 + c + 1)
                                dve.scalar_tensor_tensor(write_col[:, k:k + 1], n_before[:], FAR, this_dst, ALU.mult, ALU.add).then_inc(write_ready, 1)
                                dve.wait_ge(old_gathered, 16 * (chunk0 + c + 1))
                                if table is not None:
                                    dve.wait_ge(chunk_rows_gathered, 16 * (rows_before + c + 1))
                                if weighted:
                                    dve.wait_ge(chunk_weights_gathered, 16 * (c + 1))
                                    dve.tensor_scalar(rows[:], rows[:], row_weight[:], None, ALU.mult).then_inc(rows_scaled, 1)
                                dve.wait_ge(new_ready, chunk0 + c + 1)
                                dve.tensor_tensor(total[:], ps_new[:], old[:], ALU.add).then_inc(total_ready, 1)

                @block.tensor
                def _(pe):
                    general = pe.value_load(general_flag[0:1, 0:1], min_val=0, max_val=1)
                    with pe.If(general == 1):
                        with pe.Fori(0, NCH // 2) as i:
                            for k in range(2):
                                c = 2 * i + k
                                pe.wait_ge(wide_ready, chunk0 + c + 1)
                                pe.transpose(ps_dst[:], dst_wide[:], ident[0:CHUNK, 0:CHUNK]).then_inc(wide_turned, 1)
                                pe.wait_ge(equal_ready, chunk0 + c + 1)
                                if weighted:
                                    pe.wait_ge(rows_scaled, c + 1)
                                elif table is not None:
                                    pe.wait_ge(chunk_rows_gathered, 16 * (rows_before + c + 1))
                                pe.matmul(ps_new[:], equal[:], rows[:], start=True, stop=True).then_inc(new_ready, 1)

        def layer1():
            body, RS = 16, 16 // TS
            exists, follows, tile_loop, super_loop = loops(body)
            with ExitStack() as ctx:
                x_in = sb(ctx, "x_in", [P, RS, TS, C])
                slot_rows = sb(ctx, "slot_rows", [P, RS, TS, C])
                slot_weight = sb(ctx, "slot_weight", [P, RS, TS])
                index = sb(ctx, "index", [P, RS, TS], I32)
                pick = sb(ctx, "pick", [P, 4, P])
                scaled = sb(ctx, "scaled", [P, 2, C])
                mixed = sb(ctx, "mixed", [P, 2, C])
                turned_hi = sb(ctx, "turned_hi", [P, 2, KC, P], F32R)
                turned_lo = sb(ctx, "turned_lo", [P, 2, KC, P], F32R)
                dinv_super = sb(ctx, "dinv_super", [P, RS, TS])
                h1_out = sb(ctx, "h1_out", [P, RS, TS, H])
                ps_sum = ps(ctx, "ps_sum", [P, 2, 512])
                ps_turn = ps(ctx, "ps_turn", [P, 2, 512])
                ps_h = ps(ctx, "ps_h", [P, 2, H])
                x_loaded = [sem(f"x_loaded_{j}") for j in range(RS)]
                x_tail_loaded = sem("x_tail_loaded")
                rows_gathered = [sem(f"rows_gathered_{k}") for k in range(body)]
                h1_stored = [sem(f"h1_stored_{j}") for j in range(RS)]
                buffer_free = sem("buffer_free")
                index_ready, buffers_zeroed, pick_ready = sem("index_ready"), sem("buffers_zeroed"), sem("pick_ready")
                sum_ready, scaled_ready, mixed_ready = sem("sum_ready"), sem("scaled_ready"), sem("mixed_ready")
                turn_ready, hi_ready, lo_ready = sem("turn_ready"), sem("hi_ready"), sem("lo_ready")
                product_ready, h1_ready = sem("product_ready"), sem("h1_ready")
                dinv_super_ready = sem("dinv_super_ready")
                block = ctx.enter_context(nc.Block())

                @block.sync
                def _(sp):
                    def step(i, j):
                        if follows(i, j * TS, body):
                            sp.wait_ge(mixed_ready, body * i + TS * (j - RS + 1))
                        if isinstance(i, int) and RS * i + j == NS - 1:
                            load_tail(sp, x_in[:, j % RS], x, x_loaded[j % RS], x_tail_loaded)
                        else:
                            sp.dma_start(x_in[:, j % RS], super_rows(x, RS * i + j)).then_inc(x_loaded[j % RS], 16)
                        if follows(i, j * TS, 2 * TS):
                            store(i, j - 2)

                    def store(i, j):
                        sp.wait_ge(h1_ready, body * i + TS * (j + 1))
                        sp.dma_start(super_rows(h1_table, RS * i + j), h1_out[:, j % RS]).then_inc(h1_stored[j % RS], 16)

                    super_loop(sp, step)
                    store(0, NS - 2)
                    store(0, NS - 1)
                    for j in range(RS):
                        sp.wait_ge(h1_stored[j], 16 * ((NS - 1 - j) // RS + 1))

                @block.gpsimd
                def _(pool):
                    general = pool.value_load(general_flag[0:1, 0:1], min_val=0, max_val=1)
                    bounds = {rows: pool.to_reg(rows - 1) for rows in (N, NP)}
                    pool.memset(slot_weight[:], 0.0)
                    pool.memset(slot_rows[:], 0.0).then_inc(buffers_zeroed, 1)
                    pool.wait_ge(buffers_zeroed, 1)

                    def gather_super(i, j, table, rows):
                        pool.wait_ge(index_ready, RS * i + j + 1)
                        for g in range(TS):
                            k = TS * j + g
                            if follows(i, k, body):
                                pool.wait_ge(sum_ready, body * i + k - body + 1)
                            pool.sem_inc(buffer_free, 1)
                            for buffer, source, n in ((slot_rows[:, j % RS, g, :], table, rows), (slot_weight[:, j % RS, g:g + 1], weight_table, NP)):
                                pool.indirect_dma_start(buffer, None, source, bass.IndirectOffsetOnAxis(ap=index[:, j % RS, g:g + 1], axis=0),
                                                        bounds_check=bounds[n], oob_is_err=False).then_inc(rows_gathered[k % body], 16)

                    def step(i, j):
                        if follows(i, j * TS, body):
                            pool.wait_ge(sum_ready, body * i + TS * (j - RS + 1))
                        pool.tensor_copy(index[:, j % RS], slot_src[:, bass.ds(body * i + TS * j, TS)]).then_inc(index_ready, 1)
                        with pool.If(general == 1):
                            gather_super(i, j, sum_half, NP)
                        with pool.Else():
                            gather_super(i, j, x, N)

                    super_loop(pool, step)

                @block.vector
                def _(dve):
                    def make_pick(i, k):
                        if not exists(i, k):
                            return
                        q, g = k // TS % RS, k % TS
                        dve.wait_ge(rows_gathered[k % body], 32 * (i + k // body + 1))
                        if follows(i, k, 4):
                            dve.wait_ge(sum_ready, body * i + k - 3)
                        dve.tensor_scalar(pick[:, k % 4], iota_free[:], slot_rel[:, bass.ds(body * i + k, 1)], slot_weight[:, q, g:g + 1],
                                          ALU.is_equal, ALU.mult).then_inc(pick_ready, 1)

                    def add_own(i, k):
                        if not exists(i, k):
                            return
                        q, g = k // TS % RS, k % TS
                        if g == 0:
                            dve.wait_ge(x_loaded[q], 16 * (i + k // body + 1))
                        dve.wait_ge(scaled_ready, body * i + k + 1)
                        if follows(i, k, 2):
                            dve.wait_ge(turn_ready, body * i + k - 1)
                        dve.scalar_tensor_tensor(mixed[:, k % 2], x_in[:, q, g], self1[:, bass.ds(body * i + k, 1)], scaled[:, k % 2],
                                                 ALU.mult, ALU.add).then_inc(mixed_ready, 1)

                    def low_half(i, k):
                        if not exists(i, k):
                            return
                        dve.wait_ge(hi_ready, body * i + k + 1)
                        dve.tensor_tensor(turned_lo[:, k % 2].rearrange("p k n -> p (k n)"), ps_turn[:, k % 2, 0:C],
                                          turned_hi[:, k % 2].rearrange("p k n -> p (k n)").bitcast(F32), ALU.subtract).then_inc(lo_ready, 1)

                    def step(i, k):
                        make_pick(i, k + 3)
                        add_own(i, k + 2)
                        low_half(i, k + 1)

                    tile_loop(dve, step, ahead=3)

                @block.scalar
                def _(act):
                    def scale_sum(i, k):
                        if not exists(i, k):
                            return
                        q, g = k // TS % RS, k % TS
                        if g == 0:
                            act.activation(dinv_super[:, q], dinv[:, bass.ds(body * i + k, TS)], ACT.Copy).then_inc(dinv_super_ready, 1)
                            act.wait_ge(dinv_super_ready, RS * i + k // TS + 1)
                        act.wait_ge(sum_ready, body * i + k + 1)
                        if follows(i, k, 2):
                            act.wait_ge(mixed_ready, body * i + k - 1)
                        act.activation(scaled[:, k % 2], ps_sum[:, k % 2, 0:C], ACT.Copy,
                                       scale=dinv_super[:, q, g:g + 1]).then_inc(scaled_ready, 1)

                    def high_half(i, k):
                        if not exists(i, k):
                            return
                        act.wait_ge(turn_ready, body * i + k + 1)
                        if follows(i, k, 2):
                            act.wait_ge(product_ready, body * i + k - 1)
                        act.activation(turned_hi[:, k % 2].rearrange("p k n -> p (k n)"), ps_turn[:, k % 2, 0:C], ACT.Copy).then_inc(hi_ready, 1)

                    def rectify(i, k):
                        if not exists(i, k):
                            return
                        q, g = k // TS % RS, k % TS
                        act.wait_ge(product_ready, body * i + k + 1)
                        if g == 0 and follows(i, k, body):
                            act.wait_ge(h1_stored[q], 16 * (i + k // body))
                        act.activation(h1_out[:, q, g], ps_h[:, k % 2], ACT.Relu, scale=dinv_super[:, q, g:g + 1]).then_inc(h1_ready, 1)

                    def step(i, k):
                        scale_sum(i, k + 2)
                        high_half(i, k + 1)
                        rectify(i, k)

                    tile_loop(act, step, ahead=2)

                @block.tensor
                def _(pe):
                    def sum_slots(i, k):
                        if not exists(i, k):
                            return
                        pe.wait_ge(pick_ready, body * i + k + 1)
                        if follows(i, k, 2):
                            pe.wait_ge(scaled_ready, body * i + k - 1)
                        pe.matmul(ps_sum[:, k % 2, 0:C], pick[:, k % 4], slot_rows[:, k // TS % RS, k % TS], start=True, stop=True).then_inc(sum_ready, 1)

                    def turn(i, k):
                        if not exists(i, k):
                            return
                        pe.wait_ge(mixed_ready, body * i + k + 1)
                        if follows(i, k, 2):
                            pe.wait_ge(lo_ready, body * i + k - 1)
                        for c in range(KC):
                            last = pe.transpose(ps_turn[:, k % 2, c * P:(c + 1) * P], mixed[:, k % 2, c * P:(c + 1) * P], ident[:])
                        last.then_inc(turn_ready, 1)

                    def product(i, k):
                        if not exists(i, k):
                            return
                        if follows(i, k, 2):
                            pe.wait_ge(h1_ready, body * i + k - 1)
                        pe.matmul(ps_h[:, k % 2], ones_rows[:], b1_rows[:], start=True, stop=False)
                        pe.wait_ge(lo_ready, body * i + k + 1)
                        for c in range(KC):
                            pe.matmul(ps_h[:, k % 2], turned_hi[:, k % 2, c], w1[0][:, c], start=False, stop=False)
                            pe.matmul(ps_h[:, k % 2], turned_hi[:, k % 2, c], w1[1][:, c], start=False, stop=False)
                            last = pe.matmul(ps_h[:, k % 2], turned_lo[:, k % 2, c], w1[0][:, c], start=False, stop=(c == KC - 1))
                        last.then_inc(product_ready, 1)

                    def step(i, k):
                        sum_slots(i, k + 2)
                        turn(i, k + 1)
                        product(i, k)

                    tile_loop(pe, step, ahead=2)

        def layer2():
            body, RS = 8, 8 // TS
            exists, follows, tile_loop, super_loop = loops(body)
            with ExitStack() as ctx:
                h_in = sb(ctx, "h_in", [P, 2, TS, H])
                slot_rows = sb(ctx, "slot_rows2", [P, 2, TS, H])
                index = sb(ctx, "index2", [P, 2, TS], I32)
                pick = sb(ctx, "pick2", [P, 2, P], F32R)
                slots_hi = sb(ctx, "slots_hi", [P, 2, H], F32R)
                slots_lo = sb(ctx, "slots_lo", [P, 2, H], F32R)
                scaled = sb(ctx, "scaled2", [P, 2, H])
                mixed = sb(ctx, "mixed2", [P, 2, H])
                turned_hi = sb(ctx, "turned2_hi", [P, 2, KH, TS * P], F32R)
                turned_lo = sb(ctx, "turned2_lo", [P, 2, KH, TS * P], F32R)
                hidden = sb(ctx, "hidden", [P, 2, TS * P])
                hidden_hi = sb(ctx, "hidden_hi", [P, 2, KH, TS * P], F32R)
                hidden_lo = sb(ctx, "hidden_lo", [P, 2, KH, TS * P], F32R)
                dinv_super = sb(ctx, "dinv_super2", [P, 2, TS])
                z_out = sb(ctx, "z_out", [P, 2, TS, C])
                ps_sum = ps(ctx, "ps_sum2", [P, 2, H])
                ps_turn = ps(ctx, "ps_turn2", [P, 2, H])
                ps_h = ps(ctx, "ps_h2", [P, 2, TS * P])
                ps_z = ps(ctx, "ps_z", [P, 2, 512])
                h_loaded = [sem("h_loaded_0"), sem("h_loaded_1")]
                rows_gathered = [sem("rows2_gathered_0"), sem("rows2_gathered_1")]
                z_stored = [sem("z_stored_0"), sem("z_stored_1")]
                buffer_free = sem("buffer2_free")
                index_ready, buffers_zeroed, pick_ready = sem("index2_ready"), sem("buffers2_zeroed"), sem("pick2_ready")
                slots_hi_ready, slots_lo_ready = sem("slots_hi_ready"), sem("slots_lo_ready")
                sum_ready, scaled_ready, mixed_ready = sem("sum2_ready"), sem("scaled2_ready"), sem("mixed2_ready")
                turn_ready, hi_ready, lo_ready = sem("turn2_ready"), sem("hi2_ready"), sem("lo2_ready")
                product_ready, hidden_hi_ready, hidden_lo_ready = sem("product2_ready"), sem("hidden_hi_ready"), sem("hidden_lo_ready")
                hidden_ready = sem("hidden_ready")
                z_product_ready, z_ready = sem("z_product_ready"), sem("z_ready")
                dinv_super_ready = sem("dinv_super2_ready")
                block = ctx.enter_context(nc.Block())

                @block.sync
                def _(sp):
                    def step(i, j):
                        if follows(i, j * TS, body):
                            sp.wait_ge(mixed_ready, body * i + TS * (j - RS + 1))
                        sp.dma_start(h_in[:, j % RS], super_rows(h1_table, RS * i + j)).then_inc(h_loaded[j % RS], 16)
                        if follows(i, j * TS, 3 * TS):
                            store(i, j - 3)

                    def store(i, j):
                        sp.wait_ge(z_ready, body * i + TS * (j + 1))
                        sp.dma_start(super_rows(z_table, RS * i + j), z_out[:, j % RS]).then_inc(z_stored[j % RS], 16)

                    super_loop(sp, step, plain=2)
                    for s in range(NS - 3, NS):
                        store(0, s)
                    for j in range(RS):
                        sp.wait_ge(z_stored[j], 16 * ((NS - 1 - j) // RS + 1))

                @block.gpsimd
                def _(pool):
                    general = pool.value_load(general_flag[0:1, 0:1], min_val=0, max_val=1)
                    bounds = {rows: pool.to_reg(rows - 1) for rows in (N, NP)}
                    pool.memset(slot_rows[:], 0.0).then_inc(buffers_zeroed, 1)
                    pool.wait_ge(buffers_zeroed, 1)

                    def gather_super(i, j, table, rows):
                        pool.wait_ge(index_ready, RS * i + j + 1)
                        pool.sem_inc(buffer_free, 1)
                        for g in range(TS):
                            pool.indirect_dma_start(slot_rows[:, j % RS, g, :], None, table, bass.IndirectOffsetOnAxis(ap=index[:, j % RS, g:g + 1], axis=0),
                                                    bounds_check=bounds[rows], oob_is_err=False).then_inc(rows_gathered[j % RS], 16)

                    def step(i, j):
                        if follows(i, j * TS, body):
                            pool.wait_ge(slots_lo_ready, body * i + TS * (j - RS + 1))
                        pool.tensor_copy(index[:, j % RS], slot_src[:, bass.ds(body * i + TS * j, TS)]).then_inc(index_ready, 1)
                        with pool.If(general == 1):
                            gather_super(i, j, sum_table, NP)
                        with pool.Else():
                            gather_super(i, j, h1_table, N)

                    super_loop(pool, step)

                @block.vector
                def _(dve):
                    def make_pick(i, k):
                        if not exists(i, k):
                            return
                        if follows(i, k, 2):
                            dve.wait_ge(sum_ready, body * i + k - 1)
                        dve.tensor_scalar(pick[:, k % 2], iota_free[:], slot_rel[:, bass.ds(body * i + k, 1)], None,
                                          ALU.is_equal).then_inc(pick_ready, 1)

                    def slots_low(i, k):
                        if not exists(i, k):
                            return
                        dve.wait_ge(slots_hi_ready, body * i + k + 1)
                        dve.tensor_tensor(slots_lo[:, k % 2], slot_rows[:, k // TS % 2, k % TS], slots_hi[:, k % 2].bitcast(F32),
                                          ALU.subtract).then_inc(slots_lo_ready, 1)

                    def add_own(i, k):
                        if not exists(i, k):
                            return
                        q, g = k // TS % 2, k % TS
                        if g == 0:
                            dve.wait_ge(h_loaded[q], 16 * (i + k // body + 1))
                        dve.wait_ge(scaled_ready, body * i + k + 1)
                        if follows(i, k, 2):
                            dve.wait_ge(turn_ready, body * i + k - 1)
                        dve.scalar_tensor_tensor(mixed[:, k % 2], h_in[:, q, g], self23[:, bass.ds(body * i + k, 1)], scaled[:, k % 2],
                                                 ALU.mult, ALU.add).then_inc(mixed_ready, 1)

                    def low_half(i, k):
                        if not exists(i, k):
                            return
                        q, nodes = k // TS % 2, bass.ts(k % TS, P)
                        dve.wait_ge(hi_ready, body * i + k + 1)
                        dve.tensor_tensor(turned_lo[:, q, :, nodes], ps_turn[:, k % 2].rearrange("p (k n) -> p k n", n=P),
                                          turned_hi[:, q, :, nodes].bitcast(F32), ALU.subtract).then_inc(lo_ready, 1)

                    def hidden_low(i, k):
                        if not exists(i, k):
                            return
                        q, f = k // TS % 2, k % TS
                        dve.wait_ge(hidden_hi_ready, body * i + k + 1)
                        dve.wait_ge(hidden_ready, body * i + k + 1)
                        dve.tensor_tensor(hidden_lo[:, q, f], hidden[:, k % 2], hidden_hi[:, q, f].bitcast(F32),
                                          ALU.subtract).then_inc(hidden_lo_ready, 1)

                    def scale_z(i, k):
                        if not exists(i, k):
                            return
                        q, g = k // TS % 2, k % TS
                        if g == 0 and follows(i, k, body):
                            dve.wait_ge(z_stored[q], 16 * (i + k // body))
                        dve.wait_ge(z_product_ready, body * i + k + 1)
                        dve.tensor_scalar(z_out[:, q, g], ps_z[:, k % 2, 0:C], dinv[:, bass.ds(body * i + k, 1)], None,
                                          ALU.mult).then_inc(z_ready, 1)

                    def step(i, k):
                        make_pick(i, k + 3)
                        slots_low(i, k + 3)
                        add_own(i, k + 2)
                        low_half(i, k + 1)
                        hidden_low(i, k - TS)
                        scale_z(i, k - 2 * TS)

                    tile_loop(dve, step, ahead=3, behind=2 * TS)

                @block.scalar
                def _(act):
                    def slots_high(i, k):
                        if not exists(i, k):
                            return
                        q, g = k // TS % 2, k % TS
                        if g == 0:
                            act.wait_ge(rows_gathered[q], TS * 16 * (i + k // body + 1))
                        if follows(i, k, 2):
                            act.wait_ge(sum_ready, body * i + k - 1)
                        act.activation(slots_hi[:, k % 2], slot_rows[:, q, g], ACT.Copy).then_inc(slots_hi_ready, 1)

                    def scale_sum(i, k):
                        if not exists(i, k):
                            return
                        q, g = k // TS % 2, k % TS
                        if g == 0:
                            act.activation(dinv_super[:, q], dinv[:, bass.ds(body * i + k, TS)], ACT.Copy).then_inc(dinv_super_ready, 1)
                            act.wait_ge(dinv_super_ready, 2 * i + k // TS + 1)
                        act.wait_ge(sum_ready, body * i + k + 1)
                        if follows(i, k, 2):
                            act.wait_ge(mixed_ready, body * i + k - 1)
                        act.activation(scaled[:, k % 2], ps_sum[:, k % 2], ACT.Copy,
                                       scale=dinv_super[:, q, g:g + 1]).then_inc(scaled_ready, 1)

                    def high_half(i, k):
                        if not exists(i, k):
                            return
                        q, g = k // TS % 2, k % TS
                        act.wait_ge(turn_ready, body * i + k + 1)
                        if g == 0 and follows(i, k, 2 * TS):
                            act.wait_ge(product_ready, body * i + k - TS)
                        act.activation(turned_hi[:, q, :, bass.ts(g, P)], ps_turn[:, k % 2].rearrange("p (k n) -> p k n", n=P),
                                       ACT.Copy).then_inc(hi_ready, 1)

                    def hidden_high(i, k):
                        if not exists(i, k):
                            return
                        q, f = k // TS % 2, k % TS
                        act.wait_ge(product_ready, body * i + k + 1)
                        if f == 0 and follows(i, k, 2 * TS):
                            act.wait_ge(z_product_ready, body * i + k - TS)
                        if follows(i, k, 2):
                            act.wait_ge(hidden_lo_ready, body * i + k - 1)
                        act.activation(hidden_hi[:, q, f], ps_h[:, k % 2], ACT.Relu, bias=b2_cols[:, f:f + 1]).then_inc(hidden_hi_ready, 1)
                        act.activation(hidden[:, k % 2], ps_h[:, k % 2], ACT.Relu, bias=b2_cols[:, f:f + 1]).then_inc(hidden_ready, 1)

                    def step(i, k):
                        slots_high(i, k + 3)
                        scale_sum(i, k + 2)
                        high_half(i, k + 1)
                        hidden_high(i, k - TS)

                    tile_loop(act, step, ahead=3, behind=TS)

                @block.tensor
                def _(pe):
                    def sum_slots(i, k):
                        if not exists(i, k):
                            return
                        pe.wait_ge(pick_ready, body * i + k + 1)
                        pe.wait_ge(slots_lo_ready, body * i + k + 1)
                        if follows(i, k, 2):
                            pe.wait_ge(scaled_ready, body * i + k - 1)
                        pe.matmul(ps_sum[:, k % 2], pick[:, k % 2], slots_hi[:, k % 2], start=True, stop=False)
                        pe.matmul(ps_sum[:, k % 2], pick[:, k % 2], slots_lo[:, k % 2], start=False, stop=True).then_inc(sum_ready, 1)

                    def turn(i, k):
                        if not exists(i, k):
                            return
                        pe.wait_ge(mixed_ready, body * i + k + 1)
                        if follows(i, k, 2):
                            pe.wait_ge(lo_ready, body * i + k - 1)
                        for c in range(KH):
                            last = pe.transpose(ps_turn[:, k % 2, c * P:(c + 1) * P], mixed[:, k % 2, c * P:(c + 1) * P], ident[:])
                        last.then_inc(turn_ready, 1)

                    def product(i, k):
                        if not exists(i, k):
                            return
                        q, f = k // TS % 2, k % TS
                        if f == 0:
                            pe.wait_ge(lo_ready, body * i + k + TS)
                        if follows(i, k, 2):
                            pe.wait_ge(hidden_ready, body * i + k - 1)
                        features = slice(f * P, (f + 1) * P)
                        for c in range(KH):
                            pe.matmul(ps_h[:, k % 2], w2[0][:, c, features], turned_hi[:, q, c], start=(c == 0), stop=False)
                            pe.matmul(ps_h[:, k % 2], w2[1][:, c, features], turned_hi[:, q, c], start=False, stop=False)
                            last = pe.matmul(ps_h[:, k % 2], w2[0][:, c, features], turned_lo[:, q, c], start=False, stop=(c == KH - 1))
                        last.then_inc(product_ready, 1)

                    def product3(i, k):
                        if not exists(i, k):
                            return
                        q, nodes = k // TS % 2, slice(k % TS * P, (k % TS + 1) * P)
                        if k % TS == 0:
                            pe.wait_ge(hidden_lo_ready, body * i + k + TS)
                        if follows(i, k, 2):
                            pe.wait_ge(z_ready, body * i + k - 1)
                        for c in range(KH):
                            pe.matmul(ps_z[:, k % 2, 0:C], hidden_hi[:, q, c, nodes], w3[0][:, c], start=(c == 0), stop=False)
                            pe.matmul(ps_z[:, k % 2, 0:C], hidden_hi[:, q, c, nodes], w3[1][:, c], start=False, stop=False)
                            last = pe.matmul(ps_z[:, k % 2, 0:C], hidden_lo[:, q, c, nodes], w3[0][:, c], start=False, stop=(c == KH - 1))
                        last.then_inc(z_product_ready, 1)

                    def step(i, k):
                        sum_slots(i, k + 2)
                        turn(i, k + 1)
                        product(i, k - TS)
                        product3(i, k - 2 * TS)

                    tile_loop(pe, step, ahead=2, behind=2 * TS)

        def layer3():
            body, RS = 16, 16 // TS
            exists, follows, tile_loop, super_loop = loops(body)
            with ExitStack() as ctx:
                x_in = sb(ctx, "x_in3", [P, RS, TS, C])
                z_in = sb(ctx, "z_in", [P, RS, TS, C])
                slot_rows = sb(ctx, "slot_rows3", [P, RS, TS, C])
                index = sb(ctx, "index3", [P, RS, TS], I32)
                pick = sb(ctx, "pick3", [P, 4, P])
                own = sb(ctx, "own", [P, P])
                layer = sb(ctx, "layer", [P, 2, C])
                y = sb(ctx, "y", [P, RS, TS, C])
                halves = sb(ctx, "halves", [P, RS, TS, 6])
                gap = sb(ctx, "gap", [P, RS, TS])
                twice_mean = sb(ctx, "twice_mean", [P, RS, TS])
                spread = sb(ctx, "spread", [P, RS, TS])
                gap_square = sb(ctx, "gap_square", [P, RS, TS])
                variance = sb(ctx, "variance", [P, RS, TS])
                quarter = sb(ctx, "quarter", [P, RS, TS])
                inverse = sb(ctx, "inverse", [P, RS, TS])
                quotient = sb(ctx, "quotient", [P, RS, TS])
                half_std = sb(ctx, "half_std", [P, RS, TS])
                std = sb(ctx, "std", [P, RS, TS])
                rstd = sb(ctx, "rstd", [P, RS, TS])
                shift = sb(ctx, "shift", [P, RS, TS])
                rows_out = sb(ctx, "rows_out", [P, RS, TS, C])
                ps_sum = ps(ctx, "ps_sum3", [P, 4, 512])
                x_loaded = [sem(f"x3_loaded_{j}") for j in range(RS)]
                x_tail_loaded = sem("x3_tail_loaded")
                z_loaded = [sem(f"z_loaded_{j}") for j in range(RS)]
                rows_gathered = [sem(f"rows3_gathered_{k}") for k in range(body)]
                out_stored = [sem(f"out_stored_{j}") for j in range(RS)]
                tail_stored = sem("tail_stored")
                buffer_free = sem("buffer3_free")
                index_ready, buffers_zeroed, pick_ready = sem("index3_ready"), sem("buffers3_zeroed"), sem("pick3_ready")
                own_ready, sum_ready, layer_ready = sem("own_ready"), sem("sum3_ready"), sem("layer_ready")
                y_ready, halves_ready, links_done = sem("y_ready"), sem("halves3_ready"), sem("links_done")
                half_std_ready, out_ready = sem("half_std_ready"), sem("out_ready")
                GAP, GAP_SQUARE, VARIANCE, QUARTER, INVERSE, QUOTIENT, STD, RSTD, SHIFT = range(1, 10)
                LINKS = SHIFT
                block = ctx.enter_context(nc.Block())

                @block.sync
                def _(sp):
                    def step(i, j):
                        if follows(i, j * TS, body):
                            sp.wait_ge(y_ready, body * i + TS * (j - RS + 1))
                        sp.dma_start(z_in[:, j % RS], super_rows(z_table, RS * i + j)).then_inc(z_loaded[j % RS], 16)
                        if isinstance(i, int) and RS * i + j == NS - 1:
                            load_tail(sp, x_in[:, j % RS], x, x_loaded[j % RS], x_tail_loaded)
                        else:
                            sp.dma_start(x_in[:, j % RS], super_rows(x, RS * i + j)).then_inc(x_loaded[j % RS], 16)
                        if follows(i, j * TS, body):
                            store(i, j - RS)

                    def store(i, j):
                        sp.wait_ge(out_ready, body * i + TS * (j + 1))
                        sp.dma_start(super_rows(out, RS * i + j), rows_out[:, j % RS]).then_inc(out_stored[j % RS], 16)

                    super_loop(sp, step)
                    for s in range(NS - RS, NS - 1):
                        store(0, s)
                    sp.wait_ge(out_ready, NT)
                    r = (NS - 1) % RS
                    sp.dma_start(out[LAST:LAST + TF * P, :].rearrange("(j p) c -> p j c", p=P), rows_out[:, r, 0:TF, :]).then_inc(out_stored[r], 16)
                    sp.dma_start(out[LAST + TF * P:N, :], rows_out[0:TR, r, TF, :]).then_inc(tail_stored, 16)
                    for j in range(RS):
                        sp.wait_ge(out_stored[j], 16 * ((NS - 1 - j) // RS + 1))
                    sp.wait_ge(tail_stored, 16)

                @block.gpsimd
                def _(pool):
                    general = pool.value_load(general_flag[0:1, 0:1], min_val=0, max_val=1)
                    bounds = {rows: pool.to_reg(rows - 1) for rows in (N, NP)}
                    pool.memset(slot_rows[:], 0.0).then_inc(buffers_zeroed, 1)
                    pool.wait_ge(buffers_zeroed, 1)

                    def gather_super(i, j, table, rows):
                        pool.wait_ge(index_ready, RS * i + j + 1)
                        for g in range(TS):
                            k = TS * j + g
                            if follows(i, k, body):
                                pool.wait_ge(sum_ready, body * i + k - body + 1)
                            pool.sem_inc(buffer_free, 1)
                            pool.indirect_dma_start(slot_rows[:, j % RS, g, :], None, table, bass.IndirectOffsetOnAxis(ap=index[:, j % RS, g:g + 1], axis=0),
                                                    bounds_check=bounds[rows], oob_is_err=False).then_inc(rows_gathered[k % body], 16)

                    def step(i, j):
                        if follows(i, j * TS, body):
                            pool.wait_ge(sum_ready, body * i + TS * (j - RS + 1))
                        pool.tensor_copy(index[:, j % RS], slot_src[:, bass.ds(body * i + TS * j, TS)]).then_inc(index_ready, 1)
                        with pool.If(general == 1):
                            gather_super(i, j, sum_half, NP)
                        with pool.Else():
                            gather_super(i, j, z_table, N)

                    super_loop(pool, step)

                @block.tensor
                def _(pe):
                    def step(i, k):
                        q, g = k // TS % RS, k % TS
                        if g == 0:
                            pe.wait_ge(z_loaded[q], 16 * (i + k // body + 1))
                        if follows(i, k, 4):
                            pe.wait_ge(layer_ready, body * i + k - 3)
                        pe.matmul(ps_sum[:, k % 4, 0:C], own[:], z_in[:, q, g], start=True, stop=False)
                        pe.wait_ge(rows_gathered[k % body], 16 * (i + k // body + 1))
                        pe.wait_ge(pick_ready, body * i + k + 1)
                        pe.matmul(ps_sum[:, k % 4, 0:C], pick[:, k % 4], slot_rows[:, q, g], start=False, stop=True).then_inc(sum_ready, 1)

                    pe.wait_ge(own_ready, 1)
                    tile_loop(pe, step)

                @block.vector
                def _(dve):
                    def make_pick(i, k):
                        if not exists(i, k):
                            return
                        if follows(i, k, 4):
                            dve.wait_ge(sum_ready, body * i + k - 3)
                        dve.tensor_scalar(pick[:, k % 4], iota_free[:], slot_rel[:, bass.ds(body * i + k, 1)], None,
                                          ALU.is_equal).then_inc(pick_ready, 1)

                    def add_bias(i, k):
                        if not exists(i, k):
                            return
                        dve.wait_ge(sum_ready, body * i + k + 1)
                        if follows(i, k, 2):
                            dve.wait_ge(y_ready, body * i + k - 1)
                        dve.scalar_tensor_tensor(layer[:, k % 2], ps_sum[:, k % 4, 0:C], dinv[:, bass.ds(body * i + k, 1)], b3_all[:],
                                                 ALU.mult, ALU.add).then_inc(layer_ready, 1)

                    def add_residual(i, k):
                        if not exists(i, k):
                            return
                        q, g = k // TS % RS, k % TS
                        if g == 0:
                            dve.wait_ge(x_loaded[q], 16 * (i + k // body + 1))
                            if follows(i, k, body):
                                dve.wait_ge(out_ready, body * i + k - body + TS)
                        dve.wait_ge(layer_ready, body * i + k + 1)
                        dve.scalar_tensor_tensor(y[:, q, g], layer[:, k % 2], 0.0, x_in[:, q, g], ALU.max, ALU.add).then_inc(y_ready, 1)

                    def statistics(i, k):
                        if not exists(i, k):
                            return
                        dve.wait_ge(y_ready, body * i + k + 1)
                        dve.bn_stats(halves[:, k // TS % RS, k % TS], y[:, k // TS % RS, k % TS]).then_inc(halves_ready, 1)

                    def link(number, i, k):
                        if not exists(i, k) or k % TS != TS - 1:
                            return
                        q, s = k // TS % RS, RS * i + k // TS
                        if number == GAP:
                            dve.wait_ge(halves_ready, body * i + k + 1)
                            dve.tensor_tensor(gap[:, q], halves[:, q, :, 1], halves[:, q, :, 4], ALU.subtract).then_inc(links_done, 1)
                            dve.tensor_tensor(spread[:, q], halves[:, q, :, 2], halves[:, q, :, 5], ALU.add)
                        elif number == GAP_SQUARE:
                            dve.wait_ge(links_done, LINKS * s + GAP)
                            dve.scalar_tensor_tensor(gap_square[:, q], gap[:, q], C / 4.0, gap[:, q], ALU.mult, ALU.mult).then_inc(links_done, 1)
                            dve.tensor_tensor(twice_mean[:, q], halves[:, q, :, 1], halves[:, q, :, 4], ALU.add)
                        elif number == VARIANCE:
                            dve.wait_ge(links_done, LINKS * s + GAP_SQUARE)
                            dve.tensor_tensor(variance[:, q], gap_square[:, q], spread[:, q], ALU.add).then_inc(links_done, 1)
                        elif number == QUARTER:
                            dve.wait_ge(links_done, LINKS * s + VARIANCE)
                            dve.tensor_scalar(quarter[:, q], variance[:, q], 0.25 / C, EPS / 4, ALU.mult, ALU.add).then_inc(links_done, 1)
                        elif number == INVERSE:
                            dve.wait_ge(half_std_ready, s + 1)
                            dve.reciprocal(inverse[:, q], half_std[:, q]).then_inc(links_done, 1)
                        elif number == QUOTIENT:
                            dve.wait_ge(links_done, LINKS * s + INVERSE)
                            dve.tensor_tensor(quotient[:, q], quarter[:, q], inverse[:, q], ALU.mult).then_inc(links_done, 1)
                        elif number == STD:
                            dve.wait_ge(links_done, LINKS * s + QUOTIENT)
                            dve.tensor_tensor(std[:, q], half_std[:, q], quotient[:, q], ALU.add).then_inc(links_done, 1)
                        elif number == RSTD:
                            dve.wait_ge(links_done, LINKS * s + STD)
                            dve.reciprocal(rstd[:, q], std[:, q]).then_inc(links_done, 1)
                        elif number == SHIFT:
                            dve.wait_ge(links_done, LINKS * s + RSTD)
                            dve.scalar_tensor_tensor(shift[:, q], twice_mean[:, q], -0.5, rstd[:, q], ALU.mult, ALU.mult).then_inc(links_done, 1)

                    def step(i, k):
                        make_pick(i, k + 3)
                        link(GAP, i, k - 3)
                        link(INVERSE, i, k - 5)
                        link(SHIFT, i, k - 6)
                        add_bias(i, k)
                        link(GAP_SQUARE, i, k - 3)
                        link(QUOTIENT, i, k - 5)
                        add_residual(i, k - 1)
                        link(VARIANCE, i, k - 3)
                        link(STD, i, k - 5)
                        statistics(i, k - 2)
                        link(QUARTER, i, k - 3)
                        link(RSTD, i, k - 5)

                    dve.tensor_scalar(own[:], ident[:], own_factor[:], None, ALU.mult).then_inc(own_ready, 1)
                    tile_loop(dve, step, ahead=3, behind=6)

                @block.scalar
                def _(act):
                    def step(i, k):
                        if not exists(i, k) or k % TS != TS - 1:
                            return
                        q = k // TS % RS
                        act.wait_ge(links_done, LINKS * (RS * i + k // TS) + QUARTER)
                        if follows(i, k, body):
                            act.wait_ge(links_done, LINKS * (RS * i + k // TS - RS) + RSTD)
                        act.activation(half_std[:, q], quarter[:, q], ACT.Sqrt).then_inc(half_std_ready, 1)
                        act.wait_ge(links_done, LINKS * (RS * i + k // TS) + SHIFT)
                        if follows(i, k, body):
                            act.wait_ge(out_stored[q], 16 * (i + k // body))
                        for g in range(TS):
                            act.activation(rows_out[:, q, g], y[:, q, g], ACT.Identity, bias=shift[:, q, g:g + 1],
                                           scale=rstd[:, q, g:g + 1]).then_inc(out_ready, 1)

                    tile_loop(act, step)

        make_slots()
        general_sums("count", 0, 1, None, False, count_table)
        make_degrees()
        general_sums("one", 1, C, x, True, sum_half)
        layer1()
        general_sums("two", 2, H, h1_table, False, sum_table, rows_before=NCH)
        layer2()
        general_sums("three", 3, C, z_table, False, sum_half, rows_before=2 * NCH)
        layer3()


_INS = ["x", "src", "dst", "L0_gnn_W1", "L0_gnn_b1", "L0_gnn_W2", "L0_gnn_b2", "L0_gnn_W3", "L0_gnn_b3"]


def kernel(**inputs):
    import numpy as np
    import concourse.bacc as bacc
    from concourse.bass_utils import run_bass_kernel_spmd

    nc = bacc.Bacc("TRN2", target_bir_lowering=False, num_devices=1)
    arrays, args = {}, []
    for name in _INS:
        a = np.ascontiguousarray(inputs[name])
        arrays[f"in_{name}"] = a
        args.append(nc.dram_tensor(f"in_{name}", a.shape, mybir.dt.from_np(a.dtype), kind="ExternalInput").ap())
    args.append(nc.dram_tensor("out_rows", inputs["x"].shape, F32, kind="ExternalOutput").ap())
    gnn_kernel(nc, *args)
    r = run_bass_kernel_spmd(nc, [arrays], core_ids=[0])
    return r.results[0]["out_rows"]
```

```python
from contextlib import ExitStack

import concourse.bass as bass
from concourse import mybir

ALU = mybir.AluOpType
ACT = mybir.ActivationFunctionType
AX = mybir.AxisListType
F32 = mybir.dt.float32
F32R = mybir.dt.float32r
BF16 = mybir.dt.bfloat16
I32 = mybir.dt.int32

P = 128
TS = 4
BLK = 125
WBLK = 3
WIN = WBLK * BLK
SLOTS = 128
ROUNDS = 14
RELBIT = 16
SPLIT = 256
CHUNK = 125
EPS = 1e-5
FAR = 1000000.0


def gnn_kernel(nc, x, src, dst, W1, b1, W2, b2, W3, b3, out):
    N, C = x.shape
    E = src.shape[0]
    H = W1.shape[1]
    NS = -(-N // (TS * P))
    NT = NS * TS
    NP = NT * P
    NB = E // BLK
    NCH = E // CHUNK
    KC, KH = C // P, H // P
    TAIL = N - (NS - 1) * TS * P
    TF, TR = TAIL // P, TAIL % P
    assert E % BLK == 0 and E % (2 * CHUNK) == 0 and NB % 2 == 0 and NB <= 1024 and N < 1 << RELBIT and NS <= P
    assert TR % 16 == 0 and TR and H == 512 and C == 256

    def dram(name, shape, dt=F32):
        return nc.dram_tensor(name, shape, dt, kind="Internal").ap()

    g_table = dram("g_table", (NP, H))
    z_table = dram("z_table", (NP, C))
    dinv_table = dram("dinv_table", (NP, 1))
    weight_table = dram("weight_table", (NP, 1))
    count_table = dram("count_table", (NP, 1))
    sum_table = dram("sum_table", (NP, H))
    sum_half = sum_table.rearrange("n (a c) -> (n a) c", a=H // C)[0:NP, :]

    top = ExitStack()

    def sb(ctx, name, shape, dt=F32):
        return ctx.enter_context(nc.sbuf_tensor(name, shape, dt))

    def ps(ctx, name, shape, dt=F32):
        return ctx.enter_context(nc.psum_tensor(name, shape, dt))

    def sem(name):
        return top.enter_context(nc.semaphore(name))

    with top:
        w1 = [sb(top, f"w1_{h}", [P, KC, H], F32R) for h in ("hi", "lo")]
        w2 = [sb(top, f"w2_{h}", [P, KH, H], F32R) for h in ("hi", "lo")]
        w3 = [sb(top, f"w3_{h}", [P, KH, C], F32R) for h in ("hi", "lo")]
        b1_cols = sb(top, "b1_cols", [P, KH])
        b2_cols = sb(top, "b2_cols", [P, KH])
        b3_all = sb(top, "b3_all", [P, C])
        ident = sb(top, "ident", [P, P])
        iota_free = sb(top, "iota_free", [P, P])
        iota_part = sb(top, "iota_part", [P, 1])
        slot_src = sb(top, "slot_src", [P, NT], I32)
        slot_rel = sb(top, "slot_rel", [P, NT])
        slot_dst = sb(top, "slot_dst", [P, NT], I32)
        slot_dinv = sb(top, "slot_dinv", [P, NT])
        dinv = sb(top, "dinv", [P, NT])
        self1 = sb(top, "self1", [P, NT])
        self23 = sb(top, "self23", [P, NT])
        fast = sb(top, "fast", [P, 2])
        general_flag = sb(top, "general_flag", [P, 1], I32)
        own_factor = sb(top, "own_factor", [P, 1])


        def make_slots():
            with ExitStack() as ctx:
                first_i = sb(ctx, "first_i", [1, NB], I32)
                first_f = sb(ctx, "first_f", [1, NB])
                ones_f = sb(ctx, "ones_f", [P, P])
                stage = sb(ctx, "stage", [P, KH, H])
                stage3 = sb(ctx, "stage3", [P, KH, C])
                stage1 = sb(ctx, "stage1", [P, KC, H])
                node0 = sb(ctx, "node0", [P, TS])
                below = sb(ctx, "below", [P, NB])
                nbelow = sb(ctx, "nbelow", [P, TS])
                block_f = sb(ctx, "block_f", [P, TS])
                block_i = sb(ctx, "block_i", [P, WBLK, TS], I32)
                win_dst = sb(ctx, "win_dst", [P, TS, WIN], I32)
                win_src = sb(ctx, "win_src", [P, TS, WIN], I32)
                rel = sb(ctx, "rel", [P, TS, WIN])
                inside = sb(ctx, "inside", [P, TS, WIN])
                tmp = sb(ctx, "tmp", [P, TS, WIN])
                same = sb(ctx, "same", [P, TS, WIN])
                selfs = sb(ctx, "selfs", [P, TS, WIN])
                key = sb(ctx, "key", [P, TS, WIN])
                slot_key = sb(ctx, "slot_key", [P, TS, SLOTS])
                kept = sb(ctx, "kept", [P, TS])
                stats = sb(ctx, "stats", [P, 4])
                verdict = sb(ctx, "verdict", [P, 4])
                node_id = sb(ctx, "node_id", [P, NT])
                node_mix = sb(ctx, "node_mix", [P, NT])
                part_mix = sb(ctx, "part_mix", [P, 1])
                key_i = sb(ctx, "key_i", [P, NT], I32)
                low_i = sb(ctx, "low_i", [P, NT], I32)
                high_i = sb(ctx, "high_i", [P, NT], I32)
                src_f = sb(ctx, "src_f", [P, NT])
                rel_f = sb(ctx, "rel_f", [P, NT])
                ps_first = ps(ctx, "ps_first", [P, 2, 512])
                ps_stats = ps(ctx, "ps_stats", [P, 4])
                ps_keys = ps(ctx, "ps_keys", [P, TS, NS])
                first_loaded, weights_loaded = sem("first_loaded"), sem("weights_loaded")
                iotas_ready, first_ready = sem("iotas_ready"), sem("first_ready")
                first_spread, blocks_ready = sem("first_spread"), sem("blocks_ready")
                dst_windows, src_windows = sem("dst_windows"), sem("src_windows")
                halves_ready, stats_ready, stats_summed = sem("halves_ready"), sem("stats_ready"), sem("stats_summed")
                keys_ready, keys_turned, prep_chain = sem("keys_ready"), sem("keys_turned"), sem("prep_chain")
                rounds_done = sem("rounds_done")
                block = ctx.enter_context(nc.Block())

                @block.sync
                def _(sp):
                    with nc.allow_non_contiguous_dma(reason="the first edge of each block"):
                        sp.dma_start(first_i[:], dst.rearrange("(o b k) -> o b k", o=1, k=BLK)[:, :, 0]).then_inc(first_loaded, 16)
                    sp.dma_start(stage1[:], W1.rearrange("(k p) n -> p k n", p=P)).then_inc(weights_loaded, 16)
                    sp.dma_start(stage[:], W2.rearrange("(k p) n -> p k n", p=P)).then_inc(weights_loaded, 16)
                    sp.dma_start(stage3[:], W3.rearrange("(k p) n -> p k n", p=P)).then_inc(weights_loaded, 16)
                    sp.dma_start(b3_all[:], b3.rearrange("(o n) -> o n", o=1).to_broadcast([P, C])).then_inc(weights_loaded, 16)
                    with nc.allow_non_contiguous_dma(reason="512 biases, features on partitions"):
                        sp.dma_start(b1_cols[:], b1.rearrange("(f p) -> p f", p=P)).then_inc(weights_loaded, 16)
                        sp.dma_start(b2_cols[:], b2.rearrange("(f p) -> p f", p=P)).then_inc(weights_loaded, 16)

                @block.gpsimd
                def _(pool):
                    pool.iota(node0[:], [[P, TS]], base=0, channel_multiplier=TS * P, allow_small_or_imprecise_dtypes=True)
                    pool.iota(iota_free[:], [[1, P]], base=0, channel_multiplier=0, allow_small_or_imprecise_dtypes=True)
                    pool.iota(iota_part[:], [[0, 1]], base=0, channel_multiplier=1, allow_small_or_imprecise_dtypes=True)
                    pool.iota(node_id[:], [[P, NT]], base=0, channel_multiplier=1,
                              allow_small_or_imprecise_dtypes=True).then_inc(iotas_ready, 1)
                    pool.memset(win_dst[:], 0)
                    pool.memset(win_src[:], 0).then_inc(iotas_ready, 1)
                    pool.wait_ge(iotas_ready, 2)
                    pool.wait_ge(blocks_ready, 1)
                    for edges, window, done in ((dst, win_dst, dst_windows), (src, win_src, src_windows)):
                        blocks = edges.rearrange("(b k) -> b k", k=BLK)
                        for g in range(TS):
                            for h in range(WBLK):
                                pool.indirect_dma_start(
                                    window[0:NS, g, h * BLK:(h + 1) * BLK], None, blocks,
                                    bass.IndirectOffsetOnAxis(ap=block_i[0:NS, h, g:g + 1], axis=0),
                                    bounds_check=NB - 1, oob_is_err=False).then_inc(done, 16)

                @block.scalar
                def _(act):
                    act.wait_ge(weights_loaded, 96)
                    act.activation(w1[0][:], stage1[:], ACT.Copy)
                    act.activation(w2[0][:], stage[:], ACT.Copy)
                    act.activation(w3[0][:], stage3[:], ACT.Copy).then_inc(halves_ready, 1)

                @block.tensor
                def _(pe):
                    pe.wait_ge(first_ready, 1)
                    for h in range(2):
                        last = pe.matmul(ps_first[:, h, 0:NB // 2], ones_f[0:1, :], first_f[:, h * NB // 2:(h + 1) * NB // 2], start=True, stop=True)
                    last.then_inc(first_spread, 1)
                    pe.wait_ge(stats_ready, 1)
                    pe.matmul(ps_stats[:], ones_f[:], stats[:], start=True, stop=True).then_inc(stats_summed, 1)
                    pe.wait_ge(keys_ready, 1)
                    for g in range(TS):
                        last = pe.transpose(ps_keys[:, g, :], slot_key[0:NS, g, :], ident[0:NS, 0:NS])
                    last.then_inc(keys_turned, 1)

                @block.vector
                def _(dve):
                    count = [0]

                    def link(ins):
                        count[0] += 1
                        ins.then_inc(prep_chain, 1)
                        dve.wait_ge(prep_chain, count[0])

                    dve.memset(stats[:], 0.0)
                    dve.memset(same[:, :, 0:1], 0.0)
                    dve.memset(tmp[:, :, 0:1], 0.0)
                    dve.memset(slot_key[:], 0.0)
                    dve.memset(ones_f[:], 1.0)
                    dve.wait_ge(first_loaded, 16)
                    dve.tensor_copy(first_f[:], first_i[:]).then_inc(first_ready, 1)
                    dve.wait_ge(iotas_ready, 1)
                    link(dve.tensor_scalar(ident[:], iota_free[:], iota_part[:], None, ALU.is_equal))
                    dve.wait_ge(first_spread, 1)
                    for g in range(TS):
                        link(dve.tensor_scalar(below[:].rearrange("p (h b) -> p h b", h=2), ps_first[:, :, 0:NB // 2], node0[:, g:g + 1], None, ALU.is_lt))
                        link(dve.tensor_reduce(nbelow[:, g:g + 1], below[:], AX.X, ALU.add))
                    link(dve.tensor_scalar(block_f[:], nbelow[:], -1.0, 0.0, ALU.add, ALU.max))
                    link(dve.tensor_scalar(block_f[:], block_f[:], float(NB - WBLK), None, ALU.min))
                    for h in range(WBLK):
                        link(dve.tensor_scalar(block_i[:, h, :], block_f[:], float(h), None, ALU.add))
                    dve.sem_inc(blocks_ready, 1)
                    dve.wait_ge(halves_ready, 1)
                    dve.tensor_tensor(w1[1][:], stage1[:], w1[0][:].bitcast(F32), ALU.subtract)
                    dve.tensor_tensor(w2[1][:], stage[:], w2[0][:].bitcast(F32), ALU.subtract)
                    dve.tensor_tensor(w3[1][:], stage3[:], w3[0][:].bitcast(F32), ALU.subtract)
                    dve.wait_ge(dst_windows, 16 * WBLK * TS)
                    for g in range(TS):
                        link(dve.tensor_scalar(rel[:, g, :], win_dst[:, g, :], node0[:, g:g + 1], None, ALU.subtract))
                    link(dve.tensor_scalar(inside[:], rel[:], 0.0, None, ALU.is_ge))
                    link(dve.scalar_tensor_tensor(inside[:], rel[:], float(P), inside[:], ALU.is_lt, ALU.mult))
                    link(dve.tensor_tensor(same[:, :, 1:WIN], win_dst[:, :, 1:WIN], win_dst[:, :, 0:WIN - 1], ALU.is_equal))
                    link(dve.tensor_tensor(tmp[:, :, 1:WIN], win_dst[:, :, 1:WIN], win_dst[:, :, 0:WIN - 1], ALU.is_lt))
                    link(dve.tensor_reduce(stats[0:NS, 2:3], tmp[0:NS].rearrange("p g w -> p (g w)"), AX.X, ALU.add))
                    dve.wait_ge(src_windows, 16 * WBLK * TS)
                    link(dve.tensor_tensor(selfs[:], win_dst[:], win_src[:], ALU.is_equal))
                    link(dve.tensor_tensor(selfs[:], selfs[:], inside[:], ALU.mult))
                    link(dve.tensor_tensor_scan(tmp[:].rearrange("p g w -> p (g w)"), same[:].rearrange("p g w -> p (g w)"),
                                                selfs[:].rearrange("p g w -> p (g w)"), 0.0, ALU.mult, ALU.add))
                    link(dve.scalar_tensor_tensor(selfs[:], tmp[:], 1.0, selfs[:], ALU.is_equal, ALU.mult))
                    link(dve.tensor_reduce(stats[0:NS, 1:2], selfs[0:NS].rearrange("p g w -> p (g w)"), AX.X, ALU.add))
                    link(dve.tensor_reduce(stats[0:NS, 0:1], inside[0:NS].rearrange("p g w -> p (g w)"), AX.X, ALU.add))
                    link(dve.tensor_tensor(inside[:], inside[:], selfs[:], ALU.subtract))
                    link(dve.tensor_reduce(kept[:], inside[:], AX.X, ALU.add))
                    link(dve.tensor_scalar(kept[:], kept[:], float(8 * ROUNDS), None, ALU.is_gt))
                    link(dve.tensor_reduce(stats[0:NS, 3:4], kept[0:NS, :], AX.X, ALU.add))
                    dve.sem_inc(stats_ready, 1)
                    link(dve.scalar_tensor_tensor(key[:], rel[:], float(1 << RELBIT), win_src[:], ALU.mult, ALU.add))
                    link(dve.scalar_tensor_tensor(key[:], key[:], 1.0, inside[:], ALU.add, ALU.mult))
                    for r in range(ROUNDS):
                        for g in range(TS):
                            if r:
                                dve.wait_ge(rounds_done, TS * (2 * r - 1) + g + 1)
                            dve.max(slot_key[0:NS, g, 8 * r:8 * r + 8], key[0:NS, g, :]).then_inc(rounds_done, 1)
                        for g in range(TS):
                            if r < ROUNDS - 1:
                                dve.wait_ge(rounds_done, TS * 2 * r + g + 1)
                                dve.match_replace(key[0:NS, g, :], slot_key[0:NS, g, 8 * r:8 * r + 8], key[0:NS, g, :], 0.0).then_inc(rounds_done, 1)
                    dve.wait_ge(rounds_done, TS * (2 * ROUNDS - 1))
                    dve.sem_inc(keys_ready, 1)
                    dve.wait_ge(stats_summed, 1)
                    link(dve.tensor_scalar(verdict[:, 0:1], ps_stats[:, 0:1], float(E), None, ALU.is_equal))
                    link(dve.tensor_scalar(verdict[:, 1:2], ps_stats[:, 1:2], float(N), None, ALU.is_equal))
                    link(dve.tensor_scalar(verdict[:, 2:4], ps_stats[:, 2:4], 0.0, None, ALU.is_equal))
                    link(dve.tensor_reduce(fast[:, 0:1], verdict[:], AX.X, ALU.min))
                    link(dve.tensor_scalar(fast[:, 1:2], fast[:, 0:1], -1.0, 1.0, ALU.mult, ALU.add))
                    link(dve.tensor_copy(general_flag[:], fast[:, 1:2]))
                    dve.wait_ge(keys_turned, 1)
                    link(dve.tensor_scalar(key_i[:].rearrange("p (s g) -> p g s", g=TS), ps_keys[:], -1.0, None, ALU.add))
                    link(dve.tensor_scalar(low_i[:], key_i[:], (1 << RELBIT) - 1, None, ALU.bitwise_and))
                    link(dve.tensor_scalar(high_i[:], key_i[:], RELBIT, None, ALU.logical_shift_right))
                    link(dve.tensor_copy(src_f[:], low_i[:]))
                    link(dve.tensor_copy(rel_f[:], high_i[:]))
                    link(dve.tensor_scalar(node_mix[:], node_id[:], fast[:, 1:2], None, ALU.mult))
                    link(dve.tensor_scalar(part_mix[:], iota_part[:], fast[:, 1:2], None, ALU.mult))
                    link(dve.scalar_tensor_tensor(slot_src[:], src_f[:], fast[:, 0:1], node_mix[:], ALU.mult, ALU.add))
                    link(dve.tensor_scalar(slot_rel[:], rel_f[:], fast[:, 0:1], part_mix[:], ALU.mult, ALU.add))
                    link(dve.scalar_tensor_tensor(slot_dst[:], slot_rel[:], iota_part[:], node_id[:], ALU.subtract, ALU.add))

        def make_degrees():
            with ExitStack() as ctx:
                group = 2 * TS
                body = next(n for n in range(8, 0, -1) if NT // group % n == 0)
                one_hot = sb(ctx, "one_hot", [P, body, group, P], BF16)
                slot_rel_b = sb(ctx, "slot_rel_b", [P, NT], BF16)
                ones_b = sb(ctx, "ones_b", [P, 1], BF16)
                iota_b = sb(ctx, "iota_b", [P, P], BF16)
                degree = sb(ctx, "degree", [P, NT])
                root = sb(ctx, "root", [P, NT])
                counted = sb(ctx, "counted", [P, TS, P])
                weight = sb(ctx, "weight", [P, NT])
                turned = sb(ctx, "turned", [P, 2, TS, P])
                ps_count = ps(ctx, "ps_count", [P, NT])
                ps_general = ps(ctx, "ps_general", [P, TS, P])
                ps_dinv = ps(ctx, "ps_dinv", [P, TS, P])
                ps_weight = ps(ctx, "ps_weight", [P, TS, P])
                hot_ready, groups_counted = sem("hot_ready"), sem("groups_counted")
                general_loaded, general_turned, counts_present = sem("general_loaded"), sem("general_turned"), sem("counts_present")
                counted_zeroed, degree_ready, root_ready = sem("counted_zeroed"), sem("degree_ready"), sem("root_ready")
                dinv_ready, dinv_turned, dinv_copied = sem("dinv_ready"), sem("dinv_turned"), sem("dinv_copied")
                tables_stored, degree_chain, ones_b_ready = sem("tables_stored"), sem("degree_chain"), sem("ones_b_ready")
                block = ctx.enter_context(nc.Block())

                @block.sync
                def _(sp):
                    sp.wait_ge(counted_zeroed, 1)
                    general = sp.value_load(general_flag[0:1, 0:1], min_val=0, max_val=1)
                    with sp.If(general == 1):
                        sp.dma_start(counted[0:NS], count_table.rearrange("(s g p) o -> s g (p o)", g=TS, p=P)).then_inc(general_loaded, 16)
                        sp.wait_ge(general_loaded, 16)
                    sp.sem_inc(counts_present, 1)
                    sp.wait_ge(dinv_copied, 2)
                    for k, table in enumerate((dinv_table, weight_table)):
                        sp.dma_start(table.rearrange("(s g p) o -> s g (p o)", g=TS, p=P), turned[0:NS, k]).then_inc(tables_stored, 16)
                    sp.wait_ge(tables_stored, 32)

                @block.vector
                def _(dve):
                    count = [0]

                    def link(ins):
                        count[0] += 1
                        ins.then_inc(degree_chain, 1)
                        dve.wait_ge(degree_chain, count[0])

                    dve.memset(counted[:], 0.0).then_inc(counted_zeroed, 1)
                    dve.memset(ones_b[:], 1.0).then_inc(ones_b_ready, 1)
                    link(dve.tensor_copy(iota_b[:], iota_free[:]))
                    link(dve.tensor_copy(slot_rel_b[:], slot_rel[:]))
                    link(dve.tensor_scalar(own_factor[:], fast[:, 0:1], 1.0, None, ALU.add))

                    def hot(i, q):
                        dve.tensor_tensor(
                            one_hot[:, q], iota_b[:].rearrange("p (o n) -> p o n", o=1).to_broadcast([P, group, P]),
                            slot_rel_b[:, bass.ds(group * (body * i + q), group)].rearrange("p (g o) -> p g o", o=1).to_broadcast([P, group, P]),
                            ALU.is_equal).then_inc(hot_ready, 1)

                    for q in range(body):
                        hot(0, q)
                    with dve.Fori(1, NT // group // body) as i:
                        for q in range(body):
                            dve.wait_ge(groups_counted, body * i + q - body + 1)
                            hot(i, q)
                    dve.wait_ge(groups_counted, NT // group)
                    link(dve.tensor_scalar(degree[:], ps_count[:], fast[:, 0:1], own_factor[:], ALU.mult, ALU.add))
                    dve.wait_ge(general_turned, 1)
                    link(dve.scalar_tensor_tensor(degree[:].rearrange("p (s g) -> p g s", g=TS), ps_general[:, :, 0:NS], fast[:, 1:2],
                                                  degree[:].rearrange("p (s g) -> p g s", g=TS), ALU.mult, ALU.add))
                    dve.sem_inc(degree_ready, 1)
                    dve.wait_ge(root_ready, 1)
                    link(dve.reciprocal(dinv[:], root[:]))
                    link(dve.tensor_tensor(dinv[:], degree[:], dinv[:], ALU.mult))
                    link(dve.tensor_tensor(root[:], root[:], dinv[:], ALU.add))
                    link(dve.reciprocal(dinv[:], root[:]))
                    link(dve.tensor_scalar(dinv[:], dinv[:], 2.0, None, ALU.mult))
                    link(dve.tensor_scalar(self23[:], dinv[:], own_factor[:], None, ALU.mult))
                    link(dve.tensor_tensor(self1[:], self23[:], dinv[:], ALU.mult))
                    link(dve.tensor_scalar(weight[:], dinv[:], fast[:, 0:1], fast[:, 1:2], ALU.mult, ALU.add))
                    dve.sem_inc(dinv_ready, 1)
                    dve.wait_ge(dinv_turned, 1)
                    dve.tensor_copy(turned[0:NS, 0], ps_dinv[0:NS]).then_inc(dinv_copied, 1)
                    dve.tensor_copy(turned[0:NS, 1], ps_weight[0:NS]).then_inc(dinv_copied, 1)

                @block.scalar
                def _(act):
                    act.wait_ge(degree_ready, 1)
                    act.activation(root[:], degree[:], ACT.Sqrt).then_inc(root_ready, 1)

                @block.tensor
                def _(pe):
                    pe.wait_ge(ones_b_ready, 1)
                    with pe.Fori(0, NT // group // body) as i:
                        for q in range(body):
                            pe.wait_ge(hot_ready, body * i + q + 1)
                            for g in range(group):
                                last = pe.matmul(ps_count[:, bass.ds(group * (body * i + q) + g, 1)], one_hot[:, q, g, :], ones_b[:],
                                                 start=True, stop=True)
                            last.then_inc(groups_counted, 1)
                    pe.wait_ge(counts_present, 1)
                    for g in range(TS):
                        last = pe.transpose(ps_general[:, g, 0:NS], counted[0:NS, g, :], ident[0:NS, 0:NS])
                    last.then_inc(general_turned, 1)
                    pe.wait_ge(dinv_ready, 1)
                    for g in range(TS):
                        pe.transpose(ps_dinv[0:NS, g, :], dinv[:].rearrange("p (s g) -> p g s", g=TS)[:, g, :], ident[:])
                        last = pe.transpose(ps_weight[0:NS, g, :], weight[:].rearrange("p (s g) -> p g s", g=TS)[:, g, :], ident[:])
                    last.then_inc(dinv_turned, 1)

        def loops(body):
            supers = body // TS

            def exists(i, k):
                return not isinstance(i, int) or 0 <= body * i + k < NT

            def follows(i, k, n):
                return not isinstance(i, int) or body * i + k >= n

            def tile_loop(engine, step, ahead=0, behind=0):
                plain, end = 2 if behind else 1, (NT - ahead) // body
                for k in range(-ahead, 0):
                    step(0, k)
                for m in range(plain * body):
                    step(m // body, m % body)
                with engine.Fori(plain, end) as i:
                    for k in range(body):
                        step(i, k)
                for m in range(end * body, NT + behind):
                    step(end, m - end * body)

            def super_loop(engine, step, plain=1):
                end = (NS - 1) // supers
                for n in range(plain * supers):
                    step(n // supers, n % supers)
                with engine.Fori(plain, end) as i:
                    for j in range(supers):
                        step(i, j)
                for n in range(end * supers, NS):
                    step(end, n - end * supers)

            return exists, follows, tile_loop, super_loop

        def super_rows(table, s):
            return table[bass.ds(s * TS * P, TS * P), :].rearrange("(j p) c -> p j c", p=P)

        LAST = (NS - 1) * TS * P

        def load_tail(sp, buffer, table, loaded, tail_loaded):
            sp.dma_start(buffer[0:TR, TF, :], table[LAST + TF * P:N, :]).then_inc(tail_loaded, 16)
            sp.wait_ge(tail_loaded, 16)
            sp.dma_start(buffer[:, 0:TF, :], table[LAST:LAST + TF * P, :].rearrange("(j p) c -> p j c", p=P)).then_inc(loaded, 16)

        edges_loaded, sums_cleared, constants_ready = sem("edges_loaded"), sem("sums_cleared"), sem("constants_ready")
        wide_ready, wide_turned, equal_ready = sem("wide_ready"), sem("wide_turned"), sem("equal_ready")
        repeats_ready, count_ready, write_ready = sem("repeats_ready"), sem("count_ready"), sem("write_ready")
        chunk_rows_gathered, chunk_weights_gathered, old_gathered = sem("chunk_rows_gathered"), sem("chunk_weights_gathered"), sem("old_gathered")
        rows_scaled, new_ready = sem("rows_scaled"), sem("new_ready")
        total_ready, chunk_scattered, pool_step = sem("total_ready"), sem("chunk_scattered"), sem("pool_step")

        def general_sums(tag, turn, width, table, weighted, sums, rows_before=0):
            with ExitStack() as ctx:
                src_all = sb(ctx, f"src_all_{tag}", [CHUNK, NCH], I32)
                dst_all = sb(ctx, f"dst_all_{tag}", [CHUNK, NCH], I32)
                dst_f = sb(ctx, f"dst_f_{tag}", [CHUNK, NCH])
                zeros = sb(ctx, f"zeros_{tag}", [P, TS, width])
                before = sb(ctx, f"before_{tag}", [CHUNK, CHUNK])
                dst_wide = sb(ctx, f"dst_wide_{tag}", [CHUNK, CHUNK])
                equal = sb(ctx, f"equal_{tag}", [CHUNK, CHUNK])
                repeats = sb(ctx, f"repeats_{tag}", [CHUNK, CHUNK])
                n_before = sb(ctx, f"n_before_{tag}", [CHUNK, 1])
                src_col = sb(ctx, f"src_col_{tag}", [CHUNK, 1], I32)
                dst_col = sb(ctx, f"dst_col_{tag}", [CHUNK, 1], I32)
                write_col = sb(ctx, f"write_col_{tag}", [CHUNK, 2], I32)
                rows = sb(ctx, f"rows_{tag}", [CHUNK, width])
                row_weight = sb(ctx, f"row_weight_{tag}", [CHUNK, 1])
                old = sb(ctx, f"old_{tag}", [CHUNK, width])
                total = sb(ctx, f"total_{tag}", [CHUNK, width])
                ps_dst = ps(ctx, f"ps_dst_{tag}", [CHUNK, CHUNK])
                ps_new = ps(ctx, f"ps_new_{tag}", [CHUNK, width])
                chunk0 = turn * NCH
                block = ctx.enter_context(nc.Block())

                @block.sync
                def _(sp):
                    general = sp.value_load(general_flag[0:1, 0:1], min_val=0, max_val=1)
                    with sp.If(general == 1):
                        sp.dma_start(src_all[:], src.rearrange("(p c) -> p c", p=CHUNK)).then_inc(edges_loaded, 16)
                        sp.dma_start(dst_all[:], dst.rearrange("(p c) -> p c", p=CHUNK)).then_inc(edges_loaded, 16)
                        sp.wait_ge(constants_ready, 2 * turn + 1)
                        with sp.Fori(0, NS) as s:
                            sp.dma_start(sums[bass.ds(s * TS * P, TS * P), :].rearrange("(p j) c -> p j c", p=P), zeros[:]).then_inc(sums_cleared, 16)
                        sp.wait_ge(sums_cleared, 16 * NS * (turn + 1))

                @block.gpsimd
                def _(pool):
                    general = pool.value_load(general_flag[0:1, 0:1], min_val=0, max_val=1)
                    bounds = {n: pool.to_reg(n - 1) for n in (N, NP)}

                    def gather(buffer, source, n, index, done):
                        pool.indirect_dma_start(buffer, None, source, bass.IndirectOffsetOnAxis(ap=index, axis=0),
                                                bounds_check=bounds[n], oob_is_err=False).then_inc(done, 16)

                    with pool.If(general == 1):
                        pool.wait_ge(sums_cleared, 16 * NS * (turn + 1))
                        with pool.Fori(0, NCH // 2) as i:
                            for k in range(2):
                                pool.wait_ge(write_ready, chunk0 + 2 * i + k + 1)
                                pool.sem_inc(pool_step, 1)
                                if table is not None:
                                    gather(rows[:], table, N, src_col[:], chunk_rows_gathered)
                                if weighted:
                                    gather(row_weight[:], dinv_table, NP, src_col[:], chunk_weights_gathered)
                                gather(old[:], sums, NP, dst_col[:], old_gathered)
                                pool.wait_ge(total_ready, chunk0 + 2 * i + k + 1)
                                pool.sem_inc(pool_step, 1)
                                pool.indirect_dma_start(sums, bass.IndirectOffsetOnAxis(ap=write_col[:, k:k + 1], axis=0), total[:], None,
                                                        bounds_check=bounds[NP], oob_is_err=False).then_inc(chunk_scattered, 16)
                                pool.wait_ge(chunk_scattered, 16 * (chunk0 + 2 * i + k + 1))
                                pool.sem_inc(pool_step, 1)

                @block.vector
                def _(dve):
                    general = dve.value_load(general_flag[0:1, 0:1], min_val=0, max_val=1)
                    with dve.If(general == 1):
                        dve.memset(rows[:], 1.0)
                        dve.tensor_scalar(before[:], iota_free[0:CHUNK, 0:CHUNK], iota_part[0:CHUNK, :], None, ALU.is_lt)
                        dve.memset(zeros[:], 0.0).then_inc(constants_ready, 1)
                        dve.wait_ge(edges_loaded, 32 * (turn + 1))
                        dve.tensor_copy(dst_f[:], dst_all[:]).then_inc(constants_ready, 1)
                        dve.wait_ge(constants_ready, 2 * turn + 2)
                        with dve.Fori(0, NCH // 2) as i:
                            for k in range(2):
                                c = 2 * i + k
                                this_dst = dst_f[:, bass.ds(c, 1)]
                                dve.tensor_copy(dst_wide[:], this_dst.to_broadcast([CHUNK, CHUNK])).then_inc(wide_ready, 1)
                                dve.tensor_copy(src_col[:], src_all[:, bass.ds(c, 1)])
                                dve.tensor_copy(dst_col[:], dst_all[:, bass.ds(c, 1)])
                                dve.wait_ge(wide_turned, chunk0 + c + 1)
                                dve.tensor_scalar(equal[:], ps_dst[:], this_dst, None, ALU.is_equal).then_inc(equal_ready, 1)
                                dve.wait_ge(equal_ready, chunk0 + c + 1)
                                dve.tensor_tensor(repeats[:], equal[:], before[:], ALU.mult).then_inc(repeats_ready, 1)
                                dve.wait_ge(repeats_ready, chunk0 + c + 1)
                                dve.tensor_reduce(n_before[:], repeats[:], AX.X, ALU.add).then_inc(count_ready, 1)
                                dve.wait_ge(count_ready, chunk0 + c + 1)
                                dve.scalar_tensor_tensor(write_col[:, k:k + 1], n_before[:], FAR, this_dst, ALU.mult, ALU.add).then_inc(write_ready, 1)
                                dve.wait_ge(old_gathered, 16 * (chunk0 + c + 1))
                                if table is not None:
                                    dve.wait_ge(chunk_rows_gathered, 16 * (rows_before + c + 1))
                                if weighted:
                                    dve.wait_ge(chunk_weights_gathered, 16 * (c + 1))
                                    dve.tensor_scalar(rows[:], rows[:], row_weight[:], None, ALU.mult).then_inc(rows_scaled, 1)
                                dve.wait_ge(new_ready, chunk0 + c + 1)
                                dve.tensor_tensor(total[:], ps_new[:], old[:], ALU.add).then_inc(total_ready, 1)

                @block.tensor
                def _(pe):
                    general = pe.value_load(general_flag[0:1, 0:1], min_val=0, max_val=1)
                    with pe.If(general == 1):
                        with pe.Fori(0, NCH // 2) as i:
                            for k in range(2):
                                c = 2 * i + k
                                pe.wait_ge(wide_ready, chunk0 + c + 1)
                                pe.transpose(ps_dst[:], dst_wide[:], ident[0:CHUNK, 0:CHUNK]).then_inc(wide_turned, 1)
                                pe.wait_ge(equal_ready, chunk0 + c + 1)
                                if weighted:
                                    pe.wait_ge(rows_scaled, c + 1)
                                elif table is not None:
                                    pe.wait_ge(chunk_rows_gathered, 16 * (rows_before + c + 1))
                                pe.matmul(ps_new[:], equal[:], rows[:], start=True, stop=True).then_inc(new_ready, 1)

        def layer1():
            body, RS = 8, 8 // TS
            exists, follows, tile_loop, super_loop = loops(body)
            with ExitStack() as ctx:
                x_in = sb(ctx, "x_in1", [P, 2, TS, C])
                slot_rows = sb(ctx, "slot_rows1", [P, 2, TS, C])
                slot_weight = sb(ctx, "slot_weight", [P, 2, TS, 1])
                dinv_in = sb(ctx, "dinv_in", [P, 2, TS, 1])
                index = sb(ctx, "index1", [P, 2, TS], I32)
                index_dst = sb(ctx, "index_dst", [P, 2, TS], I32)
                pick = sb(ctx, "pick1", [P, 2, P], F32R)
                slots_hi = sb(ctx, "slots_hi", [P, 2, C], F32R)
                slots_lo = sb(ctx, "slots_lo", [P, 2, C], F32R)
                scaled = sb(ctx, "scaled", [P, 2, C])
                mixed = sb(ctx, "mixed1", [P, 2, C])
                turned_hi = sb(ctx, "turned_hi", [P, 2, KC, TS * P], F32R)
                turned_lo = sb(ctx, "turned_lo", [P, 2, KC, TS * P], F32R)
                hidden = sb(ctx, "hidden1", [P, 2, TS * P])
                hidden_hi = sb(ctx, "hidden_hi1", [P, 2, KH, TS * P], F32R)
                hidden_lo = sb(ctx, "hidden_lo1", [P, 2, KH, TS * P], F32R)
                dinv_super = sb(ctx, "dinv_super1", [P, 2, TS])
                g_out = sb(ctx, "g_out", [P, 2, TS, H])
                ps_sum = ps(ctx, "ps_sum1", [P, 2, 512])
                ps_turn = ps(ctx, "ps_turn1", [P, 2, 512])
                ps_h = ps(ctx, "ps_h", [P, 2, TS * P])
                ps_g = ps(ctx, "ps_g", [P, 2, H])
                x_loaded = [sem("x_loaded_0"), sem("x_loaded_1")]
                x_tail_loaded = sem("x_tail_loaded")
                rows_gathered = [sem("rows1_gathered_0"), sem("rows1_gathered_1")]
                dinv_gathered, dinv_kept = [sem("dinv_gathered_0"), sem("dinv_gathered_1")], sem("dinv_kept")
                index_dst_ready = sem("index_dst_ready")
                g_stored = [sem("g_stored_0"), sem("g_stored_1")]
                buffer_free = sem("buffer1_free")
                index_ready, buffers_zeroed, pick_ready = sem("index1_ready"), sem("buffers1_zeroed"), sem("pick1_ready")
                slots_hi_ready, slots_lo_ready = sem("slots_hi_ready"), sem("slots_lo_ready")
                sum_ready, scaled_ready, mixed_ready = sem("sum1_ready"), sem("scaled1_ready"), sem("mixed1_ready")
                turn_ready, hi_ready, lo_ready = sem("turn1_ready"), sem("hi1_ready"), sem("lo1_ready")
                product_ready, hidden_hi_ready, hidden_lo_ready = sem("product1_ready"), sem("hidden1_hi_ready"), sem("hidden1_lo_ready")
                hidden_ready = sem("hidden1_ready")
                g_product_ready, g_ready = sem("g_product_ready"), sem("g_ready")
                dinv_super_ready = sem("dinv_super1_ready")
                block = ctx.enter_context(nc.Block())

                @block.sync
                def _(sp):
                    def step(i, j):
                        if follows(i, j * TS, body):
                            sp.wait_ge(mixed_ready, body * i + TS * (j - RS + 1))
                        if isinstance(i, int) and RS * i + j == NS - 1:
                            load_tail(sp, x_in[:, j % RS], x, x_loaded[j % RS], x_tail_loaded)
                        else:
                            sp.dma_start(x_in[:, j % RS], super_rows(x, RS * i + j)).then_inc(x_loaded[j % RS], 16)
                        if follows(i, j * TS, 3 * TS):
                            store(i, j - 3)

                    def store(i, j):
                        sp.wait_ge(g_ready, body * i + TS * (j + 1))
                        sp.dma_start(super_rows(g_table, RS * i + j), g_out[:, j % RS]).then_inc(g_stored[j % RS], 16)

                    super_loop(sp, step, plain=2)
                    for s in range(NS - 3, NS):
                        store(0, s)
                    for j in range(RS):
                        sp.wait_ge(g_stored[j], 16 * ((NS - 1 - j) // RS + 1))

                @block.gpsimd
                def _(pool):
                    general = pool.value_load(general_flag[0:1, 0:1], min_val=0, max_val=1)
                    bounds = {rows: pool.to_reg(rows - 1) for rows in (N, NP)}

                    def gather_super(i, j, buffer, source, rows, columns, done):
                        for g in range(TS):
                            pool.indirect_dma_start(buffer[:, j % RS, g], None, source, bass.IndirectOffsetOnAxis(ap=columns[:, j % RS, g:g + 1], axis=0),
                                                    bounds_check=bounds[rows], oob_is_err=False).then_inc(done, 16)

                    def keep_dinv(i, j):
                        pool.wait_ge(dinv_gathered[j % RS], TS * 16 * (i + j // RS + 1))
                        pool.tensor_copy(slot_dinv[:, bass.ds(body * i + TS * j, TS)], dinv_in[:, j % RS, :, 0]).then_inc(dinv_kept, 1)

                    def gather_dinv(i, j):
                        if follows(i, j * TS, TS):
                            keep_dinv(i, j - 1)
                        if follows(i, j * TS, body):
                            pool.wait_ge(dinv_kept, RS * i + j - 1)
                        pool.tensor_copy(index_dst[:, j % RS], slot_dst[:, bass.ds(body * i + TS * j, TS)]).then_inc(index_dst_ready, 1)
                        pool.wait_ge(index_dst_ready, RS * i + j + 1)
                        pool.sem_inc(buffer_free, 1)
                        gather_super(i, j, dinv_in, dinv_table, NP, index_dst, dinv_gathered[j % RS])

                    def step(i, j):
                        if follows(i, j * TS, body):
                            pool.wait_ge(slots_lo_ready, body * i + TS * (j - RS + 1))
                        pool.tensor_copy(index[:, j % RS], slot_src[:, bass.ds(body * i + TS * j, TS)]).then_inc(index_ready, 1)
                        pool.wait_ge(index_ready, RS * i + j + 1)
                        if not follows(i, TS * j, body):
                            pool.wait_ge(buffers_zeroed, j + 1)
                        pool.sem_inc(buffer_free, 1)
                        with pool.If(general == 1):
                            gather_super(i, j, slot_rows, sum_half, NP, index, rows_gathered[j % RS])
                        with pool.Else():
                            gather_super(i, j, slot_rows, x, N, index, rows_gathered[j % RS])
                        gather_super(i, j, slot_weight, weight_table, NP, index, rows_gathered[j % RS])
                        if follows(i, j * TS, TS):
                            gather_dinv(i, j - 1)

                    super_loop(pool, step, plain=2)
                    gather_dinv(0, NS - 1)
                    keep_dinv(0, NS - 1)

                @block.vector
                def _(dve):
                    def make_pick(i, k):
                        if not exists(i, k):
                            return
                        if follows(i, k, 2):
                            dve.wait_ge(sum_ready, body * i + k - 1)
                        dve.tensor_scalar(pick[:, k % 2], iota_free[:], slot_rel[:, bass.ds(body * i + k, 1)], None,
                                          ALU.is_equal).then_inc(pick_ready, 1)

                    def slots_low(i, k):
                        if not exists(i, k):
                            return
                        dve.wait_ge(slots_hi_ready, body * i + k + 1)
                        q, g = k // TS % 2, k % TS
                        dve.scalar_tensor_tensor(slots_lo[:, k % 2], slot_rows[:, q, g], slot_weight[:, q, g], slots_hi[:, k % 2].bitcast(F32),
                                                 ALU.mult, ALU.subtract).then_inc(slots_lo_ready, 1)

                    def add_own(i, k):
                        if not exists(i, k):
                            return
                        q, g = k // TS % 2, k % TS
                        if g == 0:
                            dve.wait_ge(x_loaded[q], 16 * (i + k // body + 1))
                        dve.wait_ge(scaled_ready, body * i + k + 1)
                        if follows(i, k, 2):
                            dve.wait_ge(turn_ready, body * i + k - 1)
                        dve.scalar_tensor_tensor(mixed[:, k % 2], x_in[:, q, g], self1[:, bass.ds(body * i + k, 1)], scaled[:, k % 2],
                                                 ALU.mult, ALU.add).then_inc(mixed_ready, 1)

                    def low_half(i, k):
                        if not exists(i, k):
                            return
                        q, nodes = k // TS % 2, bass.ts(k % TS, P)
                        dve.wait_ge(hi_ready, body * i + k + 1)
                        dve.tensor_tensor(turned_lo[:, q, :, nodes], ps_turn[:, k % 2, 0:C].rearrange("p (k n) -> p k n", n=P),
                                          turned_hi[:, q, :, nodes].bitcast(F32), ALU.subtract).then_inc(lo_ready, 1)

                    def hidden_low(i, k):
                        if not exists(i, k):
                            return
                        q, f = k // TS % 2, k % TS
                        dve.wait_ge(hidden_hi_ready, body * i + k + 1)
                        dve.wait_ge(hidden_ready, body * i + k + 1)
                        dve.tensor_tensor(hidden_lo[:, q, f], hidden[:, k % 2], hidden_hi[:, q, f].bitcast(F32),
                                          ALU.subtract).then_inc(hidden_lo_ready, 1)

                    def scale_g(i, k):
                        if not exists(i, k):
                            return
                        q, g = k // TS % 2, k % TS
                        if g == 0 and follows(i, k, body):
                            dve.wait_ge(g_stored[q], 16 * (i + k // body))
                        dve.wait_ge(g_product_ready, body * i + k + 1)
                        dve.tensor_scalar(g_out[:, q, g], ps_g[:, k % 2], dinv[:, bass.ds(body * i + k, 1)], None,
                                          ALU.mult).then_inc(g_ready, 1)

                    def step(i, k):
                        make_pick(i, k + 3)
                        slots_low(i, k + 3)
                        add_own(i, k + 2)
                        low_half(i, k + 1)
                        hidden_low(i, k - TS)
                        scale_g(i, k - 2 * TS)

                    dve.memset(slot_weight[:], 0.0)
                    dve.memset(dinv_in[:], 0.0)
                    for j in range(RS):
                        dve.memset(slot_rows[:, j], 0.0).then_inc(buffers_zeroed, 1)
                    tile_loop(dve, step, ahead=3, behind=2 * TS)

                @block.scalar
                def _(act):
                    def slots_high(i, k):
                        if not exists(i, k):
                            return
                        q, g = k // TS % 2, k % TS
                        if g == 0:
                            act.wait_ge(rows_gathered[q], 2 * TS * 16 * (i + k // body + 1))
                        if follows(i, k, 2):
                            act.wait_ge(sum_ready, body * i + k - 1)
                        act.activation(slots_hi[:, k % 2], slot_rows[:, q, g], ACT.Copy, scale=slot_weight[:, q, g]).then_inc(slots_hi_ready, 1)

                    def scale_sum(i, k):
                        if not exists(i, k):
                            return
                        q, g = k // TS % 2, k % TS
                        if g == 0:
                            act.activation(dinv_super[:, q], dinv[:, bass.ds(body * i + k, TS)], ACT.Copy).then_inc(dinv_super_ready, 1)
                            act.wait_ge(dinv_super_ready, 2 * i + k // TS + 1)
                        act.wait_ge(sum_ready, body * i + k + 1)
                        if follows(i, k, 2):
                            act.wait_ge(mixed_ready, body * i + k - 1)
                        act.activation(scaled[:, k % 2], ps_sum[:, k % 2, 0:C], ACT.Copy,
                                       scale=dinv_super[:, q, g:g + 1]).then_inc(scaled_ready, 1)

                    def high_half(i, k):
                        if not exists(i, k):
                            return
                        q, g = k // TS % 2, k % TS
                        act.wait_ge(turn_ready, body * i + k + 1)
                        if g == 0 and follows(i, k, 2 * TS):
                            act.wait_ge(product_ready, body * i + k - TS)
                        act.activation(turned_hi[:, q, :, bass.ts(g, P)], ps_turn[:, k % 2, 0:C].rearrange("p (k n) -> p k n", n=P),
                                       ACT.Copy).then_inc(hi_ready, 1)

                    def hidden_high(i, k):
                        if not exists(i, k):
                            return
                        q, f = k // TS % 2, k % TS
                        act.wait_ge(product_ready, body * i + k + 1)
                        if f == 0 and follows(i, k, 2 * TS):
                            act.wait_ge(g_product_ready, body * i + k - TS)
                        if follows(i, k, 2):
                            act.wait_ge(hidden_lo_ready, body * i + k - 1)
                        act.activation(hidden_hi[:, q, f], ps_h[:, k % 2], ACT.Relu, bias=b1_cols[:, f:f + 1]).then_inc(hidden_hi_ready, 1)
                        act.activation(hidden[:, k % 2], ps_h[:, k % 2], ACT.Relu, bias=b1_cols[:, f:f + 1]).then_inc(hidden_ready, 1)

                    def step(i, k):
                        slots_high(i, k + 3)
                        scale_sum(i, k + 2)
                        high_half(i, k + 1)
                        hidden_high(i, k - TS)

                    tile_loop(act, step, ahead=3, behind=TS)

                @block.tensor
                def _(pe):
                    def sum_slots(i, k):
                        if not exists(i, k):
                            return
                        pe.wait_ge(pick_ready, body * i + k + 1)
                        pe.wait_ge(slots_lo_ready, body * i + k + 1)
                        if follows(i, k, 2):
                            pe.wait_ge(scaled_ready, body * i + k - 1)
                        pe.matmul(ps_sum[:, k % 2, 0:C], pick[:, k % 2], slots_hi[:, k % 2], start=True, stop=False)
                        pe.matmul(ps_sum[:, k % 2, 0:C], pick[:, k % 2], slots_lo[:, k % 2], start=False, stop=True).then_inc(sum_ready, 1)

                    def turn(i, k):
                        if not exists(i, k):
                            return
                        pe.wait_ge(mixed_ready, body * i + k + 1)
                        if follows(i, k, 2):
                            pe.wait_ge(lo_ready, body * i + k - 1)
                        for c in range(KC):
                            last = pe.transpose(ps_turn[:, k % 2, c * P:(c + 1) * P], mixed[:, k % 2, c * P:(c + 1) * P], ident[:])
                        last.then_inc(turn_ready, 1)

                    def product(i, k):
                        if not exists(i, k):
                            return
                        q, f = k // TS % 2, k % TS
                        if f == 0:
                            pe.wait_ge(lo_ready, body * i + k + TS)
                        if follows(i, k, 2):
                            pe.wait_ge(hidden_ready, body * i + k - 1)
                        features = slice(f * P, (f + 1) * P)
                        for c in range(KC):
                            pe.matmul(ps_h[:, k % 2], w1[0][:, c, features], turned_hi[:, q, c], start=(c == 0), stop=False)
                            pe.matmul(ps_h[:, k % 2], w1[1][:, c, features], turned_hi[:, q, c], start=False, stop=False)
                            last = pe.matmul(ps_h[:, k % 2], w1[0][:, c, features], turned_lo[:, q, c], start=False, stop=(c == KC - 1))
                        last.then_inc(product_ready, 1)

                    def product2(i, k):
                        if not exists(i, k):
                            return
                        q, nodes = k // TS % 2, slice(k % TS * P, (k % TS + 1) * P)
                        if k % TS == 0:
                            pe.wait_ge(hidden_lo_ready, body * i + k + TS)
                        if follows(i, k, 2):
                            pe.wait_ge(g_ready, body * i + k - 1)
                        for c in range(KH):
                            pe.matmul(ps_g[:, k % 2], hidden_hi[:, q, c, nodes], w2[0][:, c], start=(c == 0), stop=False)
                            pe.matmul(ps_g[:, k % 2], hidden_hi[:, q, c, nodes], w2[1][:, c], start=False, stop=False)
                            last = pe.matmul(ps_g[:, k % 2], hidden_lo[:, q, c, nodes], w2[0][:, c], start=False, stop=(c == KH - 1))
                        last.then_inc(g_product_ready, 1)

                    def step(i, k):
                        product(i, k - TS)
                        sum_slots(i, k + 2)
                        turn(i, k + 1)
                        product2(i, k - 2 * TS)

                    tile_loop(pe, step, ahead=2, behind=2 * TS)

        def layer2():
            body, RS = 16, 16 // TS
            exists, follows, tile_loop, super_loop = loops(body)
            with ExitStack() as ctx:
                g_in = sb(ctx, "g_in", [P, 2, TS, H])
                slot_rows = sb(ctx, "slot_rows2", [P, RS, TS, H])
                index = sb(ctx, "index2", [P, RS, TS], I32)
                pick = sb(ctx, "pick2", [P, 4, P])
                pick_one = sb(ctx, "pick_one", [P, 4, P], F32R)
                slots_hi = sb(ctx, "slots2_hi", [P, 4, SPLIT], F32R)
                slots_lo = sb(ctx, "slots2_lo", [P, 4, SPLIT], F32R)
                slot_dinv_super = sb(ctx, "slot_dinv_super", [P, 2, TS])
                dinv_super = sb(ctx, "dinv_super2", [P, 2, TS])
                mixed = sb(ctx, "mixed2", [P, 4, H])
                hidden = sb(ctx, "hidden2", [P, 4, 4 * P])
                hidden_hi = sb(ctx, "hidden2_hi", [P, 4, KH, 2 * P], F32R)
                hidden_lo = sb(ctx, "hidden2_lo", [P, 4, KH, 2 * P], F32R)
                z_out = sb(ctx, "z_out", [P, 2, TS, C])
                ps_sum = ps(ctx, "ps_sum2", [P, 2, H])
                ps_turn = ps(ctx, "ps_turn2", [P, 4, 4 * P])
                ps_z = ps(ctx, "ps_z", [P, 2, 512])
                g_loaded = [sem("g_loaded_0"), sem("g_loaded_1")]
                rows_gathered = [sem(f"rows2_gathered_{j}") for j in range(RS)]
                z_stored = [sem("z_stored_0"), sem("z_stored_1")]
                buffer_free = sem("buffer2_free")
                index_ready, buffers_zeroed, pick_ready = sem("index2_ready"), sem("buffers2_zeroed"), sem("pick2_ready")
                sum_ready, mixed_ready, turn_ready = sem("sum2_ready"), sem("mixed2_ready"), sem("turn2_ready")
                hidden_ready, hidden_lo_ready = sem("hidden2_ready"), sem("hidden2_lo_ready")
                z_product_ready, z_ready = sem("z_product_ready"), sem("z_ready")
                slots_hi_ready, slots_lo_ready = sem("slots2_hi_ready"), sem("slots2_lo_ready")
                slot_dinv_super_ready, dinv_super_ready = sem("slot_dinv_super_ready"), sem("dinv_super2_ready")
                block = ctx.enter_context(nc.Block())

                @block.sync
                def _(sp):
                    def step(i, j):
                        if follows(i, j * TS, 2 * TS):
                            sp.wait_ge(mixed_ready, body * i + TS * (j - 1))
                        sp.dma_start(g_in[:, j % 2], super_rows(g_table, RS * i + j)).then_inc(g_loaded[j % 2], 16)

                    super_loop(sp, step)
                    for j in range(2):
                        sp.wait_ge(z_stored[j], 16 * ((NS - 1 - j) // 2 + 1))

                @block.gpsimd
                def _(pool):
                    general = pool.value_load(general_flag[0:1, 0:1], min_val=0, max_val=1)
                    bounds = {rows: pool.to_reg(rows - 1) for rows in (N, NP)}
                    def gather_super(i, j, table, rows):
                        pool.wait_ge(index_ready, RS * i + j + 1)
                        if not follows(i, TS * j, body):
                            pool.wait_ge(buffers_zeroed, j + 1)
                        for g in range(TS):
                            if follows(i, TS * j, body):
                                pool.wait_ge(sum_ready, body * i + TS * j + g - body + 1)
                            pool.sem_inc(buffer_free, 1)
                            pool.indirect_dma_start(slot_rows[:, j % RS, g, :], None, table, bass.IndirectOffsetOnAxis(ap=index[:, j % RS, g:g + 1], axis=0),
                                                    bounds_check=bounds[rows], oob_is_err=False).then_inc(rows_gathered[j % RS], 16)

                    def step(i, j):
                        if follows(i, j * TS, body):
                            pool.wait_ge(sum_ready, body * i + TS * (j - RS + 1))
                        pool.tensor_copy(index[:, j % RS], slot_src[:, bass.ds(body * i + TS * j, TS)]).then_inc(index_ready, 1)
                        with pool.If(general == 1):
                            gather_super(i, j, sum_table, NP)
                        with pool.Else():
                            gather_super(i, j, g_table, N)

                    super_loop(pool, step)

                @block.tensor
                def _(pe):
                    def sum_slots(i, k):
                        if not exists(i, k):
                            return
                        q, g = k // TS % RS, k % TS
                        if g == 0:
                            pe.wait_ge(rows_gathered[q], TS * 16 * (i + k // body + 1))
                        pe.wait_ge(pick_ready, body * i + k + 1)
                        if follows(i, k, 2):
                            pe.wait_ge(mixed_ready, body * i + k - 1)
                        pe.matmul(ps_sum[:, k % 2, SPLIT:H], pick[:, k % 4], slot_rows[:, q, g, SPLIT:H], start=True, stop=True)
                        pe.wait_ge(slots_lo_ready, body * i + k + 1)
                        pe.matmul(ps_sum[:, k % 2, 0:SPLIT], pick_one[:, k % 4], slots_hi[:, k % 4], start=True, stop=False)
                        pe.matmul(ps_sum[:, k % 2, 0:SPLIT], pick_one[:, k % 4], slots_lo[:, k % 4], start=False, stop=True).then_inc(sum_ready, 1)

                    def turn(i, k):
                        if not exists(i, k):
                            return
                        pe.wait_ge(mixed_ready, body * i + k + 1)
                        if k % 2 == 0 and follows(i, k, 4):
                            pe.wait_ge(hidden_ready, body * i + k - 2)
                        for c in range(KH):
                            nodes = (c % 2 * 2 + k % 2) * P
                            last = pe.transpose(ps_turn[:, k // 2 % 2 * 2 + c // 2, nodes:nodes + P], mixed[:, k % 4, c * P:(c + 1) * P], ident[:])
                        last.then_inc(turn_ready, 1)

                    def product3(i, k):
                        if not exists(i, k):
                            return
                        r, nodes = k // 2 % 4, slice(k % 2 * P, (k % 2 + 1) * P)
                        if k % 2 == 0:
                            pe.wait_ge(hidden_lo_ready, body * i + k + 2)
                        if follows(i, k, 2):
                            pe.wait_ge(z_ready, body * i + k - 1)
                        for c in range(KH):
                            pe.matmul(ps_z[:, k % 2, 0:C], hidden_hi[:, r, c, nodes], w3[0][:, c], start=(c == 0), stop=False)
                            pe.matmul(ps_z[:, k % 2, 0:C], hidden_hi[:, r, c, nodes], w3[1][:, c], start=False, stop=False)
                            last = pe.matmul(ps_z[:, k % 2, 0:C], hidden_lo[:, r, c, nodes], w3[0][:, c], start=False, stop=(c == KH - 1))
                        last.then_inc(z_product_ready, 1)

                    def step(i, k):
                        sum_slots(i, k + 2)
                        turn(i, k + 1)
                        product3(i, k - 4)

                    tile_loop(pe, step, ahead=2, behind=4)

                @block.vector
                def _(dve):
                    def make_pick(i, k):
                        if not exists(i, k):
                            return
                        if follows(i, k, 4):
                            dve.wait_ge(sum_ready, body * i + k - 3)
                        dve.tensor_scalar(pick_one[:, k % 4], iota_free[:], slot_rel[:, bass.ds(body * i + k, 1)], None, ALU.is_equal)
                        dve.tensor_scalar(pick[:, k % 4], iota_free[:], slot_rel[:, bass.ds(body * i + k, 1)], slot_dinv[:, bass.ds(body * i + k, 1)],
                                          ALU.is_equal, ALU.mult).then_inc(pick_ready, 1)

                    def slots_low(i, k):
                        if not exists(i, k):
                            return
                        dve.wait_ge(slots_hi_ready, body * i + k + 1)
                        dve.scalar_tensor_tensor(slots_lo[:, k % 4], slot_rows[:, k // TS % RS, k % TS, 0:SPLIT], slot_dinv[:, bass.ds(body * i + k, 1)],
                                                 slots_hi[:, k % 4].bitcast(F32), ALU.mult, ALU.subtract).then_inc(slots_lo_ready, 1)

                    def add_own(i, k):
                        if not exists(i, k):
                            return
                        q, g = k // TS % 2, k % TS
                        if g == 0:
                            dve.wait_ge(g_loaded[q], 16 * (RS // 2 * i + k // TS // 2 + 1))
                        dve.wait_ge(sum_ready, body * i + k + 1)
                        if follows(i, k, 4):
                            dve.wait_ge(turn_ready, body * i + k - 3)
                        dve.scalar_tensor_tensor(mixed[:, k % 4], g_in[:, q, g], self23[:, bass.ds(body * i + k, 1)], ps_sum[:, k % 2],
                                                 ALU.mult, ALU.add).then_inc(mixed_ready, 1)

                    def hidden_low(i, k):
                        if not exists(i, k):
                            return
                        r, h = k // 2 % 4, k % 2
                        dve.wait_ge(hidden_ready, body * i + k + 1)
                        dve.tensor_tensor(hidden_lo[:, r, 2 * h:2 * h + 2].rearrange("p c n -> p (c n)"), hidden[:, k % 4],
                                          hidden_hi[:, r, 2 * h:2 * h + 2].rearrange("p c n -> p (c n)").bitcast(F32),
                                          ALU.subtract).then_inc(hidden_lo_ready, 1)

                    def step(i, k):
                        make_pick(i, k + 4)
                        slots_low(i, k + 3)
                        add_own(i, k + 2)
                        hidden_low(i, k - 1)

                    for j in range(RS):
                        dve.memset(slot_rows[:, j], 0.0).then_inc(buffers_zeroed, 1)
                    tile_loop(dve, step, ahead=4, behind=1)

                @block.scalar
                def _(act):
                    def slots_high(i, k):
                        if not exists(i, k):
                            return
                        q, g = k // TS % RS, k % TS
                        if g == 0:
                            if follows(i, k, 2 * TS):
                                act.wait_ge(slots_hi_ready, body * i + k - TS)
                            act.activation(slot_dinv_super[:, q % 2], slot_dinv[:, bass.ds(body * i + k, TS)], ACT.Copy).then_inc(slot_dinv_super_ready, 1)
                            act.wait_ge(slot_dinv_super_ready, RS * i + k // TS + 1)
                            act.wait_ge(rows_gathered[q], TS * 16 * (i + k // body + 1))
                        if follows(i, k, 4):
                            act.wait_ge(sum_ready, body * i + k - 3)
                        act.activation(slots_hi[:, k % 4], slot_rows[:, q, g, 0:SPLIT], ACT.Copy,
                                       scale=slot_dinv_super[:, q % 2, g:g + 1]).then_inc(slots_hi_ready, 1)

                    def store(i, j):
                        act.wait_ge(z_ready, body * i + TS * (j + 1))
                        act.dma_start(super_rows(z_table, RS * i + j), z_out[:, j % 2]).then_inc(z_stored[j % 2], 16)

                    def scale_z(i, k):
                        if not exists(i, k):
                            return
                        q, g = k // TS % 2, k % TS
                        if g == 0:
                            if follows(i, k, TS):
                                store(i, k // TS - 1)
                            act.activation(dinv_super[:, q], dinv[:, bass.ds(body * i + k, TS)], ACT.Copy).then_inc(dinv_super_ready, 1)
                            act.wait_ge(dinv_super_ready, RS * i + k // TS + 1)
                            if follows(i, k, 2 * TS):
                                act.wait_ge(z_stored[q], 16 * (RS // 2 * i + k // TS // 2))
                        act.wait_ge(z_product_ready, body * i + k + 1)
                        act.activation(z_out[:, q, g], ps_z[:, k % 2, 0:C], ACT.Copy, scale=dinv_super[:, q, g:g + 1]).then_inc(z_ready, 1)

                    def rectify(i, k):
                        if not exists(i, k):
                            return
                        r, h = k // 2 % 4, k % 2
                        act.wait_ge(turn_ready, body * i + k - h + 2)
                        if h == 0 and follows(i, k, 8):
                            act.wait_ge(z_product_ready, body * i + k - 6)
                        if follows(i, k, 4):
                            act.wait_ge(hidden_lo_ready, body * i + k - 3)
                        for whole in (False, True):
                            for b in range(2):
                                f = 2 * h + b
                                rows = hidden[:, k % 4, b * 2 * P:(b + 1) * 2 * P] if whole else hidden_hi[:, r, f]
                                last = act.activation(rows, ps_turn[:, k // 2 % 2 * 2 + h, b * 2 * P:(b + 1) * 2 * P], ACT.Relu,
                                                      bias=b2_cols[:, f:f + 1])
                        last.then_inc(hidden_ready, 1)

                    def step(i, k):
                        slots_high(i, k + 4)
                        rectify(i, k - 1)
                        scale_z(i, k - 4)

                    tile_loop(act, step, ahead=4, behind=4)
                    store(0, NS - 1)

        def layer3():
            body, RS = 16, 16 // TS
            exists, follows, tile_loop, super_loop = loops(body)
            with ExitStack() as ctx:
                x_in = sb(ctx, "x_in3", [P, RS, TS, C])
                z_in = sb(ctx, "z_in", [P, RS, TS, C])
                slot_rows = sb(ctx, "slot_rows3", [P, RS, TS, C])
                index = sb(ctx, "index3", [P, RS, TS], I32)
                pick = sb(ctx, "pick3", [P, 4, P])
                own = sb(ctx, "own", [P, P])
                layer = sb(ctx, "layer", [P, 2, C])
                y = sb(ctx, "y", [P, RS, TS, C])
                halves = sb(ctx, "halves", [P, RS, TS, 6])
                gap = sb(ctx, "gap", [P, RS, TS])
                twice_mean = sb(ctx, "twice_mean", [P, RS, TS])
                spread = sb(ctx, "spread", [P, RS, TS])
                gap_square = sb(ctx, "gap_square", [P, RS, TS])
                variance = sb(ctx, "variance", [P, RS, TS])
                quarter = sb(ctx, "quarter", [P, RS, TS])
                inverse = sb(ctx, "inverse", [P, RS, TS])
                quotient = sb(ctx, "quotient", [P, RS, TS])
                half_std = sb(ctx, "half_std", [P, RS, TS])
                std = sb(ctx, "std", [P, RS, TS])
                rstd = sb(ctx, "rstd", [P, RS, TS])
                shift = sb(ctx, "shift", [P, RS, TS])
                rows_out = sb(ctx, "rows_out", [P, RS, TS, C])
                ps_sum = ps(ctx, "ps_sum3", [P, 4, 512])
                x_loaded = [sem(f"x3_loaded_{j}") for j in range(RS)]
                x_tail_loaded = sem("x3_tail_loaded")
                z_loaded = [sem(f"z_loaded_{j}") for j in range(RS)]
                rows_gathered = [sem(f"rows3_gathered_{k}") for k in range(body)]
                out_stored = [sem(f"out_stored_{j}") for j in range(RS)]
                tail_stored = sem("tail_stored")
                buffer_free = sem("buffer3_free")
                index_ready, buffers_zeroed, pick_ready = sem("index3_ready"), sem("buffers3_zeroed"), sem("pick3_ready")
                own_ready, sum_ready, layer_ready = sem("own_ready"), sem("sum3_ready"), sem("layer_ready")
                y_ready, halves_ready, links_done = sem("y_ready"), sem("halves3_ready"), sem("links_done")
                half_std_ready, out_ready = sem("half_std_ready"), sem("out_ready")
                GAP, GAP_SQUARE, VARIANCE, QUARTER, INVERSE, QUOTIENT, STD, RSTD, SHIFT = range(1, 10)
                LINKS = SHIFT
                block = ctx.enter_context(nc.Block())

                @block.sync
                def _(sp):
                    def step(i, j):
                        if follows(i, j * TS, body):
                            sp.wait_ge(y_ready, body * i + TS * (j - RS + 1))
                        sp.dma_start(z_in[:, j % RS], super_rows(z_table, RS * i + j)).then_inc(z_loaded[j % RS], 16)
                        if isinstance(i, int) and RS * i + j == NS - 1:
                            load_tail(sp, x_in[:, j % RS], x, x_loaded[j % RS], x_tail_loaded)
                        else:
                            sp.dma_start(x_in[:, j % RS], super_rows(x, RS * i + j)).then_inc(x_loaded[j % RS], 16)
                        if follows(i, j * TS, body):
                            store(i, j - RS)

                    def store(i, j):
                        sp.wait_ge(out_ready, body * i + TS * (j + 1))
                        sp.dma_start(super_rows(out, RS * i + j), rows_out[:, j % RS]).then_inc(out_stored[j % RS], 16)

                    super_loop(sp, step)
                    for s in range(NS - RS, NS - 1):
                        store(0, s)
                    sp.wait_ge(out_ready, NT)
                    r = (NS - 1) % RS
                    sp.dma_start(out[LAST:LAST + TF * P, :].rearrange("(j p) c -> p j c", p=P), rows_out[:, r, 0:TF, :]).then_inc(out_stored[r], 16)
                    sp.dma_start(out[LAST + TF * P:N, :], rows_out[0:TR, r, TF, :]).then_inc(tail_stored, 16)
                    for j in range(RS):
                        sp.wait_ge(out_stored[j], 16 * ((NS - 1 - j) // RS + 1))
                    sp.wait_ge(tail_stored, 16)

                @block.gpsimd
                def _(pool):
                    general = pool.value_load(general_flag[0:1, 0:1], min_val=0, max_val=1)
                    bounds = {rows: pool.to_reg(rows - 1) for rows in (N, NP)}
                    def gather_super(i, j, table, rows):
                        pool.wait_ge(index_ready, RS * i + j + 1)
                        if not follows(i, TS * j, body):
                            pool.wait_ge(buffers_zeroed, j + 1)
                        for g in range(TS):
                            k = TS * j + g
                            if follows(i, k, body):
                                pool.wait_ge(sum_ready, body * i + k - body + 1)
                            pool.sem_inc(buffer_free, 1)
                            pool.indirect_dma_start(slot_rows[:, j % RS, g, :], None, table, bass.IndirectOffsetOnAxis(ap=index[:, j % RS, g:g + 1], axis=0),
                                                    bounds_check=bounds[rows], oob_is_err=False).then_inc(rows_gathered[k % body], 16)

                    def step(i, j):
                        if follows(i, j * TS, body):
                            pool.wait_ge(sum_ready, body * i + TS * (j - RS + 1))
                        pool.tensor_copy(index[:, j % RS], slot_src[:, bass.ds(body * i + TS * j, TS)]).then_inc(index_ready, 1)
                        with pool.If(general == 1):
                            gather_super(i, j, sum_half, NP)
                        with pool.Else():
                            gather_super(i, j, z_table, N)

                    super_loop(pool, step)

                @block.tensor
                def _(pe):
                    def step(i, k):
                        q, g = k // TS % RS, k % TS
                        if g == 0:
                            pe.wait_ge(z_loaded[q], 16 * (i + k // body + 1))
                        if follows(i, k, 4):
                            pe.wait_ge(layer_ready, body * i + k - 3)
                        pe.matmul(ps_sum[:, k % 4, 0:C], own[:], z_in[:, q, g], start=True, stop=False)
                        pe.wait_ge(rows_gathered[k % body], 16 * (i + k // body + 1))
                        pe.wait_ge(pick_ready, body * i + k + 1)
                        pe.matmul(ps_sum[:, k % 4, 0:C], pick[:, k % 4], slot_rows[:, q, g], start=False, stop=True).then_inc(sum_ready, 1)

                    pe.wait_ge(own_ready, 1)
                    tile_loop(pe, step)

                @block.vector
                def _(dve):
                    def make_pick(i, k):
                        if not exists(i, k):
                            return
                        if follows(i, k, 4):
                            dve.wait_ge(sum_ready, body * i + k - 3)
                        dve.tensor_scalar(pick[:, k % 4], iota_free[:], slot_rel[:, bass.ds(body * i + k, 1)], None,
                                          ALU.is_equal).then_inc(pick_ready, 1)

                    def add_bias(i, k):
                        if not exists(i, k):
                            return
                        dve.wait_ge(sum_ready, body * i + k + 1)
                        if follows(i, k, 2):
                            dve.wait_ge(y_ready, body * i + k - 1)
                        dve.scalar_tensor_tensor(layer[:, k % 2], ps_sum[:, k % 4, 0:C], dinv[:, bass.ds(body * i + k, 1)], b3_all[:],
                                                 ALU.mult, ALU.add).then_inc(layer_ready, 1)

                    def add_residual(i, k):
                        if not exists(i, k):
                            return
                        q, g = k // TS % RS, k % TS
                        if g == 0:
                            dve.wait_ge(x_loaded[q], 16 * (i + k // body + 1))
                            if follows(i, k, body):
                                dve.wait_ge(out_ready, body * i + k - body + TS)
                        dve.wait_ge(layer_ready, body * i + k + 1)
                        dve.scalar_tensor_tensor(y[:, q, g], layer[:, k % 2], 0.0, x_in[:, q, g], ALU.max, ALU.add).then_inc(y_ready, 1)

                    def statistics(i, k):
                        if not exists(i, k):
                            return
                        dve.wait_ge(y_ready, body * i + k + 1)
                        dve.bn_stats(halves[:, k // TS % RS, k % TS], y[:, k // TS % RS, k % TS]).then_inc(halves_ready, 1)

                    def link(number, i, k):
                        if not exists(i, k) or k % TS != TS - 1:
                            return
                        q, s = k // TS % RS, RS * i + k // TS
                        if number == GAP:
                            dve.wait_ge(halves_ready, body * i + k + 1)
                            dve.tensor_tensor(gap[:, q], halves[:, q, :, 1], halves[:, q, :, 4], ALU.subtract).then_inc(links_done, 1)
                            dve.tensor_tensor(spread[:, q], halves[:, q, :, 2], halves[:, q, :, 5], ALU.add)
                        elif number == GAP_SQUARE:
                            dve.wait_ge(links_done, LINKS * s + GAP)
                            dve.scalar_tensor_tensor(gap_square[:, q], gap[:, q], C / 4.0, gap[:, q], ALU.mult, ALU.mult).then_inc(links_done, 1)
                            dve.tensor_tensor(twice_mean[:, q], halves[:, q, :, 1], halves[:, q, :, 4], ALU.add)
                        elif number == VARIANCE:
                            dve.wait_ge(links_done, LINKS * s + GAP_SQUARE)
                            dve.tensor_tensor(variance[:, q], gap_square[:, q], spread[:, q], ALU.add).then_inc(links_done, 1)
                        elif number == QUARTER:
                            dve.wait_ge(links_done, LINKS * s + VARIANCE)
                            dve.tensor_scalar(quarter[:, q], variance[:, q], 0.25 / C, EPS / 4, ALU.mult, ALU.add).then_inc(links_done, 1)
                        elif number == INVERSE:
                            dve.wait_ge(half_std_ready, s + 1)
                            dve.reciprocal(inverse[:, q], half_std[:, q]).then_inc(links_done, 1)
                        elif number == QUOTIENT:
                            dve.wait_ge(links_done, LINKS * s + INVERSE)
                            dve.tensor_tensor(quotient[:, q], quarter[:, q], inverse[:, q], ALU.mult).then_inc(links_done, 1)
                        elif number == STD:
                            dve.wait_ge(links_done, LINKS * s + QUOTIENT)
                            dve.tensor_tensor(std[:, q], half_std[:, q], quotient[:, q], ALU.add).then_inc(links_done, 1)
                        elif number == RSTD:
                            dve.wait_ge(links_done, LINKS * s + STD)
                            dve.reciprocal(rstd[:, q], std[:, q]).then_inc(links_done, 1)
                        elif number == SHIFT:
                            dve.wait_ge(links_done, LINKS * s + RSTD)
                            dve.scalar_tensor_tensor(shift[:, q], twice_mean[:, q], -0.5, rstd[:, q], ALU.mult, ALU.mult).then_inc(links_done, 1)

                    def step(i, k):
                        make_pick(i, k + 3)
                        link(GAP, i, k - 3)
                        link(INVERSE, i, k - 5)
                        link(SHIFT, i, k - 6)
                        add_bias(i, k)
                        link(GAP_SQUARE, i, k - 3)
                        link(QUOTIENT, i, k - 5)
                        add_residual(i, k - 1)
                        link(VARIANCE, i, k - 3)
                        link(STD, i, k - 5)
                        statistics(i, k - 2)
                        link(QUARTER, i, k - 3)
                        link(RSTD, i, k - 5)

                    for j in range(RS):
                        dve.memset(slot_rows[:, j], 0.0).then_inc(buffers_zeroed, 1)
                    dve.tensor_scalar(own[:], ident[:], own_factor[:], None, ALU.mult).then_inc(own_ready, 1)
                    tile_loop(dve, step, ahead=3, behind=6)

                @block.scalar
                def _(act):
                    def step(i, k):
                        if not exists(i, k) or k % TS != TS - 1:
                            return
                        q = k // TS % RS
                        act.wait_ge(links_done, LINKS * (RS * i + k // TS) + QUARTER)
                        if follows(i, k, body):
                            act.wait_ge(links_done, LINKS * (RS * i + k // TS - RS) + RSTD)
                        act.activation(half_std[:, q], quarter[:, q], ACT.Sqrt).then_inc(half_std_ready, 1)
                        act.wait_ge(links_done, LINKS * (RS * i + k // TS) + SHIFT)
                        if follows(i, k, body):
                            act.wait_ge(out_stored[q], 16 * (i + k // body))
                        for g in range(TS):
                            act.activation(rows_out[:, q, g], y[:, q, g], ACT.Identity, bias=shift[:, q, g:g + 1],
                                           scale=rstd[:, q, g:g + 1]).then_inc(out_ready, 1)

                    tile_loop(act, step)

        make_slots()
        general_sums("count", 0, 1, None, False, count_table)
        make_degrees()
        general_sums("one", 1, C, x, True, sum_half)
        layer1()
        general_sums("two", 2, H, g_table, False, sum_table, rows_before=NCH)
        layer2()
        general_sums("three", 3, C, z_table, False, sum_half, rows_before=2 * NCH)
        layer3()


_INS = ["x", "src", "dst", "L0_gnn_W1", "L0_gnn_b1", "L0_gnn_W2", "L0_gnn_b2", "L0_gnn_W3", "L0_gnn_b3"]


def kernel(**inputs):
    import numpy as np
    import concourse.bacc as bacc
    from concourse.bass_utils import run_bass_kernel_spmd

    nc = bacc.Bacc("TRN2", target_bir_lowering=False, num_devices=1)
    arrays, args = {}, []
    for name in _INS:
        a = np.ascontiguousarray(inputs[name])
        arrays[f"in_{name}"] = a
        args.append(nc.dram_tensor(f"in_{name}", a.shape, mybir.dt.from_np(a.dtype), kind="ExternalInput").ap())
    args.append(nc.dram_tensor("out_rows", inputs["x"].shape, F32, kind="ExternalOutput").ap())
    gnn_kernel(nc, *args)
    r = run_bass_kernel_spmd(nc, [arrays], core_ids=[0])
    return r.results[0]["out_rows"]
```
